# Optimizing a Trainium2 kernel written in Bass

```python
import numpy as np
import jax
import jax.numpy as jnp

def _softmax(x, axis=-1):
    return jax.nn.softmax(x, axis=axis)

def _gelu(x):
    return jax.nn.gelu(x, approximate=True)

def _silu(x):
    return jax.nn.silu(x)

def _sigmoid(x):
    return jax.nn.sigmoid(x)

def _layernorm(x, axis=-1, eps=1e-05):
    m = jnp.mean(x, axis=axis, keepdims=True)
    v = jnp.var(x, axis=axis, keepdims=True)
    return (x - m) / jnp.sqrt(v + eps)

def _scatter_add(tgt, idx, src, axis=0):
    return tgt.at[idx].add(src)

def _segment_sum(src, seg, n):
    return jax.ops.segment_sum(src, seg, n)
kernel_name = 'mk_flamingo_gated_d4_seqx_r8_1d4021'

def setup_inputs(seed: int=0):
    np.random.seed(seed)
    _w = jnp.asarray

    def _rec_inputs():
        import jax
        import jax.numpy as jnp
        _rk = jax.random.key(seed)
        x = -0.0002928 + 1 * jax.random.normal(jax.random.fold_in(_rk, 1), (8, 256, 128), jnp.float32)
        _lenS = 256 - jax.random.randint(jax.random.fold_in(_rk, 7), (8,), 0, max(1, 256 // 4) + 1, jnp.int32)
        _lenS2 = 256 - jax.random.randint(jax.random.fold_in(_rk, 8), (8,), 0, max(1, 256 // 4) + 1, jnp.int32)
        _ctx_1024P = jax.random.normal(jax.random.fold_in(_rk, 11), (8, 16, 128), jnp.float32)
        _ctx_1024c = jax.random.dirichlet(jax.random.fold_in(_rk, 511), 0.3 * jnp.ones((16,), jnp.float32), (8, 256))
        _ctx_1024t = jnp.einsum('bsk,bkd->bsd', _ctx_1024c, _ctx_1024P)
        _ctx_1024t = _ctx_1024t * jax.lax.rsqrt(jnp.mean(jnp.square(_ctx_1024t)) + 1e-12) * 0.953939
        ctx_1024 = -1.39393e-06 + 0.999914 * (_ctx_1024t + 0.3 * jax.random.normal(jax.random.fold_in(_rk, 611), (8, 256, 128), jnp.float32))
        _validS = jnp.arange(256)[None, :] < _lenS[:, None]
        _validS2 = jnp.arange(256)[None, :] < _lenS2[:, None]
        _causal = jnp.tril(jnp.ones((256, 256), dtype=bool))
        mask_BxS2_if0 = jnp.where(jnp.ones((8, 256), dtype=bool), 0, 1).astype(jnp.int32)
        _g = jax.random.normal(jax.random.fold_in(_rk, 9001), (2, 4), jnp.float32)
        _g = jnp.sign(_g) * jnp.maximum(jnp.abs(_g), 1.0) + (_g == 0) * 1.0
        g_xattn = _g[0]
        g_ffn = _g[1]
        return (x, ctx_1024, mask_BxS2_if0, g_xattn, g_ffn)
    x, ctx_1024, mask_BxS2_if0, g_xattn, g_ffn = _rec_inputs()

    def _L0_xattn_setup():
        import jax, jax.numpy as jnp
        import numpy as np
        import math
        N_HEADS = 16
        D_MODEL = 128
        CONTEXT_LEN = 256
        D_HEAD = D_MODEL // N_HEADS
        BATCH = 2

        def _rope_tables(context_len, d_head):
            position = jnp.arange(context_len, dtype=jnp.float32)[:, None]
            div = 10000.0 ** (jnp.arange(0, d_head, 2, dtype=jnp.float32) / d_head)
            div = jnp.repeat(div, 2, axis=-1)
            ang = position / div
            return (jnp.cos(ang), jnp.sin(ang))

        def _apply_rope(x, cos, sin):
            ce = cos[None, None, :, 0::2]
            se = sin[None, None, :, 0::2]
            xe = x[..., 0::2]
            xo = x[..., 1::2]
            re = xe * ce - xo * se
            ro = xe * se + xo * ce
            return jnp.stack([re, ro], axis=-1).reshape(x.shape)
        key = jax.random.key(seed)
        kq, kk, kv = jax.random.split(key, 3)
        shape = (BATCH, CONTEXT_LEN, D_MODEL)
        return {'q': jax.random.normal(kq, shape, dtype=jnp.float32), 'k': jax.random.normal(kk, shape, dtype=jnp.float32), 'v': jax.random.normal(kv, shape, dtype=jnp.float32)}
    _L0_xattn_all = _L0_xattn_setup()
    _L0_xattn_in = {k: v for k, v in _L0_xattn_all.items() if k in ()}
    del _L0_xattn_all

    def _L0_ffn_setup():
        import jax, jax.numpy as jnp
        import numpy as np
        NUM_NOD = 6
        MAX_PREV = 5
        NUM_EDGE = 20
        D = 128
        H = 8
        LN_EPS = 1e-06

        def _layernorm(x, g, b):
            mu = jnp.mean(x, axis=-1, keepdims=True)
            var = jnp.mean(jnp.square(x - mu), axis=-1, keepdims=True)
            return (x - mu) * jax.lax.rsqrt(var + LN_EPS) * g + b

        def _mha(q, k, v, wq, wk, wv, wo):
            B, S, d = q.shape
            dh = d // H
            qh = (q @ wq).reshape(B, S, H, dh)
            kh = (k @ wk).reshape(B, S, H, dh)
            vh = (v @ wv).reshape(B, S, H, dh)
            scores = jnp.einsum('bqhd,bkhd->bhqk', qh, kh) / jnp.sqrt(jnp.asarray(dh, q.dtype))
            attn = jax.nn.softmax(scores, axis=-1)
            ctx = jnp.einsum('bhqk,bkhd->bqhd', attn, vh).reshape(B, S, d)
            return ctx @ wo
        key = jax.random.key(seed)
        ks = jax.random.split(key, 12)
        B, S = (8, 128)
        scale = 1.0 / np.sqrt(D)
        return {'inputs': jax.random.normal(ks[0], (B, S, D), jnp.float32), 'ew': jax.random.uniform(ks[1], (NUM_NOD, 3), jnp.float32), 'act_w': jax.random.uniform(ks[2], (NUM_NOD,), jnp.float32), 'We': jax.random.normal(ks[3], (NUM_EDGE, D, D), jnp.float32) * scale, 'be': jnp.zeros((NUM_EDGE, D), jnp.float32), 'Wq': jax.random.normal(ks[4], (NUM_NOD, D, D), jnp.float32) * scale, 'Wk': jax.random.normal(ks[5], (NUM_NOD, D, D), jnp.float32) * scale, 'Wv': jax.random.normal(ks[6], (NUM_NOD, D, D), jnp.float32) * scale, 'Wo': jax.random.normal(ks[7], (NUM_NOD, D, D), jnp.float32) * scale, 'ln_g': jnp.ones((D,), jnp.float32), 'ln_b': jnp.zeros((D,), jnp.float32)}
    _L0_ffn_all = _L0_ffn_setup()
    _L0_ffn_in = {k: v for k, v in _L0_ffn_all.items() if k in ('ew', 'act_w', 'We', 'be', 'Wq', 'Wk', 'Wv', 'Wo', 'ln_g', 'ln_b')}
    del _L0_ffn_all

    def _L1_xattn_setup():
        import jax, jax.numpy as jnp
        import numpy as np
        DIM = 128
        NUM_HEADS = 16
        DIM_HEAD = 64
        INNER = NUM_HEADS * DIM_HEAD
        SCALE = DIM_HEAD ** (-0.5)

        def _layernorm(x, gamma, beta, eps=1e-05):
            mu = jnp.mean(x, axis=-1, keepdims=True)
            var = jnp.mean(jnp.square(x - mu), axis=-1, keepdims=True)
            return (x - mu) * jax.lax.rsqrt(var + eps) * gamma + beta
        key = jax.random.key(seed)
        ks = jax.random.split(key, 8)
        B, SQ, SK = (2, 256, 512)
        x = jax.random.normal(ks[0], (B, SQ, DIM), dtype=jnp.float32)
        context = jax.random.normal(ks[1], (B, SK, DIM), dtype=jnp.float32)
        ln_gamma = jnp.ones((DIM,), jnp.float32)
        ln_beta = jnp.zeros((DIM,), jnp.float32)
        w_q = jax.random.normal(ks[2], (DIM, INNER), dtype=jnp.float32) / np.sqrt(DIM)
        w_kv = jax.random.normal(ks[3], (DIM, 2 * INNER), dtype=jnp.float32) / np.sqrt(DIM)
        w_out = jax.random.normal(ks[4], (INNER, DIM), dtype=jnp.float32) / np.sqrt(INNER)
        b_out = jnp.zeros((DIM,), jnp.float32)
        gate = jnp.array([0.5], jnp.float32)
        return {'x': x, 'context': context, 'ln_gamma': ln_gamma, 'ln_beta': ln_beta, 'w_q': w_q, 'w_kv': w_kv, 'w_out': w_out, 'b_out': b_out, 'gate': gate}
    _L1_xattn_all = _L1_xattn_setup()
    _L1_xattn_in = {k: v for k, v in _L1_xattn_all.items() if k in ('ln_gamma', 'ln_beta', 'w_q', 'w_kv', 'w_out', 'b_out', 'gate')}
    del _L1_xattn_all

    def _L1_ffn_setup():
        import jax, jax.numpy as jnp
        import numpy as np
        QMAX = 127.0

        def _ste_round(v):
            return v + jax.lax.stop_gradient(jnp.round(v) - v)

        def _act_fake_quant(x, clip_factor):
            scale = jax.nn.sigmoid(clip_factor) * jnp.max(jnp.abs(x)) / QMAX
            return jnp.clip(_ste_round(x / scale), -QMAX - 1.0, QMAX) * scale

        def _weight_fake_quant(w):
            scale = jnp.max(jnp.abs(w), axis=1, keepdims=True) / QMAX
            return jnp.clip(_ste_round(w / scale), -QMAX - 1.0, QMAX) * scale
        key = jax.random.key(seed)
        k1, k2, k3, k4 = jax.random.split(key, 4)
        B, S, H, I = (8, 1024, 128, 352)
        return {'x': jax.random.normal(k1, (B, S, H), dtype=jnp.float32), 'clip_x': jnp.full((1,), 4.0, dtype=jnp.float32), 'clip_down': jnp.full((1,), 4.0, dtype=jnp.float32), 'w_gate': jax.random.normal(k2, (I, H), dtype=jnp.float32) * 0.02, 'w_up': jax.random.normal(k3, (I, H), dtype=jnp.float32) * 0.02, 'w_down': jax.random.normal(k4, (H, I), dtype=jnp.float32) * 0.02}
    _L1_ffn_all = _L1_ffn_setup()
    _L1_ffn_in = {k: v for k, v in _L1_ffn_all.items() if k in ('clip_x', 'clip_down', 'w_gate', 'w_up', 'w_down')}
    del _L1_ffn_all

    def _L2_xattn_setup():
        import jax, jax.numpy as jnp
        import numpy as np
        HEAD_NUM = 16
        NEG_INF = float('-inf')
        key = jax.random.key(seed)
        ks = jax.random.split(key, 4)
        B, S, D = (4, 256, 128)
        q = jax.random.normal(ks[0], (B, S, D), dtype=jnp.float32)
        k = jax.random.normal(ks[1], (B, S, D), dtype=jnp.float32)
        v = jax.random.normal(ks[2], (B, S, D), dtype=jnp.float32)
        W = jax.random.normal(ks[3], (D, D), dtype=jnp.float32) / np.sqrt(D)
        b = jnp.zeros((D,), dtype=jnp.float32)
        mask = jnp.zeros((B, S), dtype=jnp.int32)
        return {'q': q, 'k': k, 'v': v, 'W': W, 'b': b, 'mask': mask}
    _L2_xattn_all = _L2_xattn_setup()
    _L2_xattn_in = {k: v for k, v in _L2_xattn_all.items() if k in ('W', 'b')}
    del _L2_xattn_all

    def _L2_ffn_setup():
        import jax, jax.numpy as jnp
        import numpy as np
        EPS = 1e-08

        def _ste(x, q):
            return x + jax.lax.stop_gradient(q - x)

        def quant_act_uint8(x):
            s = jax.lax.stop_gradient(jnp.maximum(jnp.max(x), EPS)) / 255.0
            q = jnp.clip(jnp.round(x / s), 0.0, 255.0) * s
            return (_ste(x, q), s)

        def quant_weight_int8_perchannel(w):
            s = jax.lax.stop_gradient(jnp.maximum(jnp.max(jnp.abs(w), axis=1, keepdims=True), EPS)) / 127.0
            q = jnp.clip(jnp.round(w / s), -128.0, 127.0) * s
            return (_ste(w, q), s[:, 0])

        def quant_bias_int32(b, s_in, s_w):
            s = jax.lax.stop_gradient(s_in * s_w)
            q = jnp.round(b / s) * s
            return _ste(b, q)

        def quant_linear(x, w, b):
            xq, s_in = quant_act_uint8(x)
            wq, s_w = quant_weight_int8_perchannel(w)
            bq = quant_bias_int32(b, s_in, s_w)
            return jnp.einsum('btd,fd->btf', xq, wq) + bq
        key = jax.random.key(seed)
        k1, k2, k3, k4, k5 = jax.random.split(key, 5)
        B, S, D, F = (4, 256, 128, 512)
        return {'x': jax.random.normal(k1, (B, S, D), dtype=jnp.float32), 'w1': jax.random.normal(k2, (F, D), dtype=jnp.float32) * (1.0 / np.sqrt(D)), 'b1': jax.random.normal(k3, (F,), dtype=jnp.float32) * 0.01, 'w2': jax.random.normal(k4, (D, F), dtype=jnp.float32) * (1.0 / np.sqrt(F)), 'b2': jax.random.normal(k5, (D,), dtype=jnp.float32) * 0.01}
    _L2_ffn_all = _L2_ffn_setup()
    _L2_ffn_in = {k: v for k, v in _L2_ffn_all.items() if k in ('w1', 'b1', 'w2', 'b2')}
    del _L2_ffn_all

    def _L3_xattn_setup():
        import jax, jax.numpy as jnp
        import numpy as np
        D_MODEL = 128
        NUM_HEADS = 16
        HEAD_DIM = D_MODEL // NUM_HEADS
        key = jax.random.key(seed)
        ks = jax.random.split(key, 10)
        B, SQ, SKV = (4, 256, 256)
        s = 1.0 / np.sqrt(D_MODEL)
        return {'query': jax.random.normal(ks[0], (B, SQ, D_MODEL), jnp.float32), 'key_value': jax.random.normal(ks[1], (B, SKV, D_MODEL), jnp.float32), 'Wq': jax.random.normal(ks[2], (D_MODEL, D_MODEL), jnp.float32) * s, 'bq': jnp.zeros((D_MODEL,), jnp.float32), 'Wk': jax.random.normal(ks[3], (D_MODEL, D_MODEL), jnp.float32) * s, 'bk': jnp.zeros((D_MODEL,), jnp.float32), 'Wv': jax.random.normal(ks[4], (D_MODEL, D_MODEL), jnp.float32) * s, 'bv': jnp.zeros((D_MODEL,), jnp.float32), 'Wo': jax.random.normal(ks[5], (D_MODEL, D_MODEL), jnp.float32) * s, 'bo': jnp.zeros((D_MODEL,), jnp.float32)}
    _L3_xattn_all = _L3_xattn_setup()
    _L3_xattn_in = {k: v for k, v in _L3_xattn_all.items() if k in ('Wq', 'bq', 'Wk', 'bk', 'Wv', 'bv', 'Wo', 'bo')}
    del _L3_xattn_all

    def _L3_ffn_setup():
        import jax, jax.numpy as jnp
        import numpy as np
        E, G, TOPK = (32, 16, 2)
        HID, INTER, A_INTER = (128, 256, 128)
        CAP_FACTOR = 1.25
        SCALE = 0.05

        def _stats(x):
            mean = x.mean(-1, keepdims=True)
            std = jnp.std(x, axis=-1, keepdims=True, ddof=1)
            mn = x.min(-1, keepdims=True)
            mx = x.max(-1, keepdims=True)
            l2 = jnp.linalg.norm(x, axis=-1, keepdims=True)
            sp = (jnp.abs(x) < 1e-06).astype(x.dtype).mean(-1, keepdims=True)
            return jnp.concatenate([mean, std, mn, mx, l2, sp], -1)
        key = jax.random.key(seed)
        ks = jax.random.split(key, 8)
        B, N = (4, 128)
        s = lambda k, shape, sc: jax.random.normal(k, shape, jnp.float32) * sc
        return {'x': jax.random.normal(ks[0], (B, N, HID), jnp.float32), 'r1_w': s(ks[1], (HID // 2, HID + 6), 0.02), 'r1_b': jnp.zeros((HID // 2,), jnp.float32), 'r2_w': s(ks[2], (E, HID // 2), 0.02), 'w_up': s(ks[3], (E, 2 * INTER, HID), 0.02), 'w_down': s(ks[4], (E, HID, INTER), 0.02), 'a_up': s(ks[5], (G, 2 * A_INTER, HID), 0.02), 'a_down': s(ks[6], (G, HID, A_INTER), 0.02)}
    _L3_ffn_all = _L3_ffn_setup()
    _L3_ffn_in = {k: v for k, v in _L3_ffn_all.items() if k in ('r1_w', 'r1_b', 'r2_w', 'w_up', 'w_down', 'a_up', 'a_down')}
    del _L3_ffn_all
    return {'x': x, 'ctx_1024': ctx_1024, 'mask_BxS2_if0': mask_BxS2_if0, 'g_xattn': g_xattn, 'g_ffn': g_ffn, 'L0_ffn_ew': _L0_ffn_in['ew'], 'L0_ffn_act_w': _L0_ffn_in['act_w'], 'L0_ffn_We': _L0_ffn_in['We'], 'L0_ffn_be': _L0_ffn_in['be'], 'L0_ffn_Wq': _L0_ffn_in['Wq'], 'L0_ffn_Wk': _L0_ffn_in['Wk'], 'L0_ffn_Wv': _L0_ffn_in['Wv'], 'L0_ffn_Wo': _L0_ffn_in['Wo'], 'L0_ffn_ln_g': _L0_ffn_in['ln_g'], 'L0_ffn_ln_b': _L0_ffn_in['ln_b'], 'L1_xattn_ln_gamma': _L1_xattn_in['ln_gamma'], 'L1_xattn_ln_beta': _L1_xattn_in['ln_beta'], 'L1_xattn_w_q': _L1_xattn_in['w_q'], 'L1_xattn_w_kv': _L1_xattn_in['w_kv'], 'L1_xattn_w_out': _L1_xattn_in['w_out'], 'L1_xattn_b_out': _L1_xattn_in['b_out'], 'L1_xattn_gate': _L1_xattn_in['gate'], 'L1_ffn_clip_x': _L1_ffn_in['clip_x'], 'L1_ffn_clip_down': _L1_ffn_in['clip_down'], 'L1_ffn_w_gate': _L1_ffn_in['w_gate'], 'L1_ffn_w_up': _L1_ffn_in['w_up'], 'L1_ffn_w_down': _L1_ffn_in['w_down'], 'L2_xattn_W': _L2_xattn_in['W'], 'L2_xattn_b': _L2_xattn_in['b'], 'L2_ffn_w1': _L2_ffn_in['w1'], 'L2_ffn_b1': _L2_ffn_in['b1'], 'L2_ffn_w2': _L2_ffn_in['w2'], 'L2_ffn_b2': _L2_ffn_in['b2'], 'L3_xattn_Wq': _L3_xattn_in['Wq'], 'L3_xattn_bq': _L3_xattn_in['bq'], 'L3_xattn_Wk': _L3_xattn_in['Wk'], 'L3_xattn_bk': _L3_xattn_in['bk'], 'L3_xattn_Wv': _L3_xattn_in['Wv'], 'L3_xattn_bv': _L3_xattn_in['bv'], 'L3_xattn_Wo': _L3_xattn_in['Wo'], 'L3_xattn_bo': _L3_xattn_in['bo'], 'L3_ffn_r1_w': _L3_ffn_in['r1_w'], 'L3_ffn_r1_b': _L3_ffn_in['r1_b'], 'L3_ffn_r2_w': _L3_ffn_in['r2_w'], 'L3_ffn_w_up': _L3_ffn_in['w_up'], 'L3_ffn_w_down': _L3_ffn_in['w_down'], 'L3_ffn_a_up': _L3_ffn_in['a_up'], 'L3_ffn_a_down': _L3_ffn_in['a_down']}

def reference(x, ctx_1024, mask_BxS2_if0, g_xattn, g_ffn, L0_ffn_ew, L0_ffn_act_w, L0_ffn_We, L0_ffn_be, L0_ffn_Wq, L0_ffn_Wk, L0_ffn_Wv, L0_ffn_Wo, L0_ffn_ln_g, L0_ffn_ln_b, L1_xattn_ln_gamma, L1_xattn_ln_beta, L1_xattn_w_q, L1_xattn_w_kv, L1_xattn_w_out, L1_xattn_b_out, L1_xattn_gate, L1_ffn_clip_x, L1_ffn_clip_down, L1_ffn_w_gate, L1_ffn_w_up, L1_ffn_w_down, L2_xattn_W, L2_xattn_b, L2_ffn_w1, L2_ffn_b1, L2_ffn_w2, L2_ffn_b2, L3_xattn_Wq, L3_xattn_bq, L3_xattn_Wk, L3_xattn_bk, L3_xattn_Wv, L3_xattn_bv, L3_xattn_Wo, L3_xattn_bo, L3_ffn_r1_w, L3_ffn_r1_b, L3_ffn_r2_w, L3_ffn_w_up, L3_ffn_w_down, L3_ffn_a_up, L3_ffn_a_down):
    import jax
    import jax.numpy as jnp

    def _L0_xattn_ref(q, k, v):
        import jax, jax.numpy as jnp
        import numpy as np
        import math
        N_HEADS = 16
        D_MODEL = 128
        CONTEXT_LEN = 256
        D_HEAD = D_MODEL // N_HEADS
        BATCH = 2

        def _rope_tables(context_len, d_head):
            position = jnp.arange(context_len, dtype=jnp.float32)[:, None]
            div = 10000.0 ** (jnp.arange(0, d_head, 2, dtype=jnp.float32) / d_head)
            div = jnp.repeat(div, 2, axis=-1)
            ang = position / div
            return (jnp.cos(ang), jnp.sin(ang))

        def _apply_rope(x, cos, sin):
            ce = cos[None, None, :, 0::2]
            se = sin[None, None, :, 0::2]
            xe = x[..., 0::2]
            xo = x[..., 1::2]
            re = xe * ce - xo * se
            ro = xe * se + xo * ce
            return jnp.stack([re, ro], axis=-1).reshape(x.shape)
        b, s, d_model = q.shape
        qh = q.reshape(b, N_HEADS, s, D_HEAD)
        kh = k.reshape(b, N_HEADS, s, D_HEAD)
        vh = v.reshape(b, N_HEADS, s, D_HEAD)
        cos, sin = _rope_tables(CONTEXT_LEN, D_HEAD)
        cos, sin = (cos[:s], sin[:s])
        qh = _apply_rope(qh, cos, sin)
        kh = _apply_rope(kh, cos, sin)
        scale = 1.0 / math.sqrt(D_HEAD)
        scores = jnp.einsum('bhqd,bhkd->bhqk', qh, kh) * scale
        causal = jnp.tril(jnp.ones((s, s), dtype=bool))
        scores = jnp.where(causal[None, None], scores, jnp.finfo(scores.dtype).min)
        attn = jax.nn.softmax(scores, axis=-1)
        out = jnp.einsum('bhqk,bhkd->bhqd', attn, vh)
        return out.reshape(b, s, d_model)

    def _L0_ffn_ref(inputs, ew, act_w, We, be, Wq, Wk, Wv, Wo, ln_g, ln_b):
        import jax, jax.numpy as jnp
        import numpy as np
        NUM_NOD = 6
        MAX_PREV = 5
        NUM_EDGE = 20
        D = 128
        H = 8
        LN_EPS = 1e-06

        def _layernorm(x, g, b):
            mu = jnp.mean(x, axis=-1, keepdims=True)
            var = jnp.mean(jnp.square(x - mu), axis=-1, keepdims=True)
            return (x - mu) * jax.lax.rsqrt(var + LN_EPS) * g + b

        def _mha(q, k, v, wq, wk, wv, wo):
            B, S, d = q.shape
            dh = d // H
            qh = (q @ wq).reshape(B, S, H, dh)
            kh = (k @ wk).reshape(B, S, H, dh)
            vh = (v @ wv).reshape(B, S, H, dh)
            scores = jnp.einsum('bqhd,bkhd->bhqk', qh, kh) / jnp.sqrt(jnp.asarray(dh, q.dtype))
            attn = jax.nn.softmax(scores, axis=-1)
            ctx = jnp.einsum('bhqk,bkhd->bqhd', attn, vh).reshape(B, S, d)
            return ctx @ wo
        nodes = {-1: inputs}
        lind = 0
        for c in range(NUM_NOD):
            nsrc = min(c + 1, MAX_PREV)
            snode = c - nsrc
            eq, ek, ev = (lind + nsrc - 1, lind, lind + nsrc // 2)
            in_q, in_k, in_v = (c - 1, snode, snode + nsrc // 2)
            q = ew[c, 0] * (nodes[in_q] @ We[eq] + be[eq])
            k = ew[c, 1] * (nodes[in_k] @ We[ek] + be[ek])
            v = ew[c, 2] * (nodes[in_v] @ We[ev] + be[ev])
            o = _mha(q, k, v, Wq[c], Wk[c], Wv[c], Wo[c])
            nodes[c] = act_w[c] * o + q
            lind += nsrc
        out = nodes[NUM_NOD - 1]
        return _layernorm(out, ln_g, ln_b)

    def _L1_xattn_ref(x, context, ln_gamma, ln_beta, w_q, w_kv, w_out, b_out, gate):
        import jax, jax.numpy as jnp
        import numpy as np
        DIM = 128
        NUM_HEADS = 16
        DIM_HEAD = 64
        INNER = NUM_HEADS * DIM_HEAD
        SCALE = DIM_HEAD ** (-0.5)

        def _layernorm(x, gamma, beta, eps=1e-05):
            mu = jnp.mean(x, axis=-1, keepdims=True)
            var = jnp.mean(jnp.square(x - mu), axis=-1, keepdims=True)
            return (x - mu) * jax.lax.rsqrt(var + eps) * gamma + beta
        B, SQ, _ = x.shape
        SK = context.shape[1]
        xn = _layernorm(x, ln_gamma, ln_beta)
        q = (xn @ w_q).reshape(B, SQ, NUM_HEADS, DIM_HEAD)
        kv = context @ w_kv
        k, v = jnp.split(kv, 2, axis=-1)
        k = k.reshape(B, SK, NUM_HEADS, DIM_HEAD)
        v = v.reshape(B, SK, NUM_HEADS, DIM_HEAD)
        scores = jnp.einsum('bqhd,bkhd->bhqk', q * SCALE, k)
        attn = jax.nn.softmax(scores, axis=-1)
        out = jnp.einsum('bhqk,bkhd->bqhd', attn, v).reshape(B, SQ, INNER)
        out = out @ w_out + b_out
        return out * jnp.tanh(gate[0])

    def _L1_ffn_ref(x, clip_x, clip_down, w_gate, w_up, w_down):
        import jax, jax.numpy as jnp
        import numpy as np
        QMAX = 127.0

        def _ste_round(v):
            return v + jax.lax.stop_gradient(jnp.round(v) - v)

        def _act_fake_quant(x, clip_factor):
            scale = jax.nn.sigmoid(clip_factor) * jnp.max(jnp.abs(x)) / QMAX
            return jnp.clip(_ste_round(x / scale), -QMAX - 1.0, QMAX) * scale

        def _weight_fake_quant(w):
            scale = jnp.max(jnp.abs(w), axis=1, keepdims=True) / QMAX
            return jnp.clip(_ste_round(w / scale), -QMAX - 1.0, QMAX) * scale
        xq = _act_fake_quant(x, clip_x[0])
        gate = jnp.einsum('bsh,ih->bsi', xq, _weight_fake_quant(w_gate))
        up = jnp.einsum('bsh,ih->bsi', xq, _weight_fake_quant(w_up))
        h = _act_fake_quant(jax.nn.silu(gate) * up, clip_down[0])
        return jnp.einsum('bsi,hi->bsh', h, _weight_fake_quant(w_down))

    def _L2_xattn_ref(q, k, v, W, b, mask):
        import jax, jax.numpy as jnp
        import numpy as np
        HEAD_NUM = 16
        NEG_INF = float('-inf')
        B, Sq, D = q.shape
        Sk = k.shape[1]
        H = HEAD_NUM
        dh = D // H
        qh = q.reshape(B, Sq, H, dh).transpose(0, 2, 1, 3)
        kh = k.reshape(B, Sk, H, dh).transpose(0, 2, 1, 3)
        vh = v.reshape(B, Sk, H, dh).transpose(0, 2, 1, 3)
        scores = jnp.einsum('bhqd,bhkd->bhqk', qh, kh) / jnp.sqrt(jnp.asarray(dh, q.dtype))
        pad = mask[:, None, None, :]
        causal = jnp.triu(jnp.ones((Sq, Sk), dtype=jnp.int32), k=1)[None, None]
        merged = jnp.where(causal == 1, causal, pad)
        scores = jnp.where(merged == 1, NEG_INF, scores)
        attn = jax.nn.softmax(scores, axis=-1)
        out = jnp.einsum('bhqk,bhkd->bhqd', attn, vh)
        out = out.transpose(0, 2, 1, 3).reshape(B, Sq, D)
        return out @ W.T + b

    def _L2_ffn_ref(x, w1, b1, w2, b2):
        import jax, jax.numpy as jnp
        import numpy as np
        EPS = 1e-08

        def _ste(x, q):
            return x + jax.lax.stop_gradient(q - x)

        def quant_act_uint8(x):
            s = jax.lax.stop_gradient(jnp.maximum(jnp.max(x), EPS)) / 255.0
            q = jnp.clip(jnp.round(x / s), 0.0, 255.0) * s
            return (_ste(x, q), s)

        def quant_weight_int8_perchannel(w):
            s = jax.lax.stop_gradient(jnp.maximum(jnp.max(jnp.abs(w), axis=1, keepdims=True), EPS)) / 127.0
            q = jnp.clip(jnp.round(w / s), -128.0, 127.0) * s
            return (_ste(w, q), s[:, 0])

        def quant_bias_int32(b, s_in, s_w):
            s = jax.lax.stop_gradient(s_in * s_w)
            q = jnp.round(b / s) * s
            return _ste(b, q)

        def quant_linear(x, w, b):
            xq, s_in = quant_act_uint8(x)
            wq, s_w = quant_weight_int8_perchannel(w)
            bq = quant_bias_int32(b, s_in, s_w)
            return jnp.einsum('btd,fd->btf', xq, wq) + bq
        h = jax.nn.relu(quant_linear(x, w1, b1))
        return quant_linear(h, w2, b2)

    def _L3_xattn_ref(query, key_value, Wq, bq, Wk, bk, Wv, bv, Wo, bo):
        import jax, jax.numpy as jnp
        import numpy as np
        D_MODEL = 128
        NUM_HEADS = 16
        HEAD_DIM = D_MODEL // NUM_HEADS
        B, SQ, _ = query.shape
        SKV = key_value.shape[1]
        H, Dh = (NUM_HEADS, HEAD_DIM)
        Q = (query @ Wq.T + bq).reshape(B, SQ, H, Dh).transpose(0, 2, 1, 3)
        K = (key_value @ Wk.T + bk).reshape(B, SKV, H, Dh).transpose(0, 2, 1, 3)
        V = (key_value @ Wv.T + bv).reshape(B, SKV, H, Dh).transpose(0, 2, 1, 3)
        scale = jnp.asarray(np.sqrt(Dh), query.dtype)
        scores = jnp.einsum('bhqd,bhkd->bhqk', Q, K) / scale
        weights = jax.nn.softmax(scores, axis=-1)
        attn = jnp.einsum('bhqk,bhkd->bhqd', weights, V)
        attn = attn.transpose(0, 2, 1, 3).reshape(B, SQ, H * Dh)
        return attn @ Wo.T + bo

    def _L3_ffn_ref(x, r1_w, r1_b, r2_w, w_up, w_down, a_up, a_down):
        import jax, jax.numpy as jnp
        import numpy as np
        E, G, TOPK = (32, 16, 2)
        HID, INTER, A_INTER = (128, 256, 128)
        CAP_FACTOR = 1.25
        SCALE = 0.05

        def _stats(x):
            mean = x.mean(-1, keepdims=True)
            std = jnp.std(x, axis=-1, keepdims=True, ddof=1)
            mn = x.min(-1, keepdims=True)
            mx = x.max(-1, keepdims=True)
            l2 = jnp.linalg.norm(x, axis=-1, keepdims=True)
            sp = (jnp.abs(x) < 1e-06).astype(x.dtype).mean(-1, keepdims=True)
            return jnp.concatenate([mean, std, mn, mx, l2, sp], -1)
        B, N, C = x.shape
        xf = x.reshape(-1, C)
        T = xf.shape[0]
        cap = int(CAP_FACTOR * T / E)
        ri = jnp.concatenate([xf, _stats(xf)], -1)
        h = jax.nn.gelu(ri @ r1_w.T + r1_b, approximate=False)
        probs = jax.nn.softmax(h @ r2_w.T, -1)
        topp, topi = jax.lax.top_k(probs, TOPK)
        wnorm = topp / topp.sum(-1, keepdims=True)
        eids = jnp.arange(E)
        hit = topi[..., None] == eids
        routed = hit.any(1)
        Wc = jnp.where(hit, wnorm[..., None], 0.0).sum(1)
        score = jnp.where(routed, probs, -jnp.inf)
        idx = jnp.argsort(-score, axis=0)[:cap].T
        valid = jnp.take_along_axis(routed.T, idx, 1)
        w = jnp.take_along_axis(Wc.T, idx, 1) * valid
        xe = xf[idx]
        up = jnp.einsum('eci,eji->ecj', xe, w_up)
        gate, upv = jnp.split(up, 2, axis=-1)
        hact = jax.nn.silu(gate) * upv
        ye = jnp.einsum('ecj,eoj->eco', hact, w_down)
        out = jnp.zeros((T, C), xf.dtype).at[idx.reshape(-1)].add((w[..., None] * ye).reshape(-1, C))
        Wmask = jnp.zeros((T, E), xf.dtype).at[idx, eids[:, None]].add(w)
        gw = SCALE * Wmask.reshape(T, G, E // G).sum(-1)
        aup = jnp.einsum('tc,gjc->tgj', xf, a_up)
        ag, av = jnp.split(aup, 2, axis=-1)
        ah = jax.nn.silu(ag) * av
        ay = jnp.einsum('tgj,goj->tgo', ah, a_down)
        out = out + jnp.einsum('tg,tgo->to', gw, ay)
        return out.reshape(B, N, C)
    x = x + jnp.tanh(g_xattn[0]) * _L0_xattn_ref(_layernorm(x, axis=-1), ctx_1024, ctx_1024)
    x = x + jnp.tanh(g_ffn[0]) * _L0_ffn_ref(_layernorm(x, axis=-1), L0_ffn_ew, L0_ffn_act_w, L0_ffn_We, L0_ffn_be, L0_ffn_Wq, L0_ffn_Wk, L0_ffn_Wv, L0_ffn_Wo, L0_ffn_ln_g, L0_ffn_ln_b)
    x = x + jnp.tanh(g_xattn[1]) * _L1_xattn_ref(_layernorm(x, axis=-1), ctx_1024, L1_xattn_ln_gamma, L1_xattn_ln_beta, L1_xattn_w_q, L1_xattn_w_kv, L1_xattn_w_out, L1_xattn_b_out, L1_xattn_gate)
    x = x + jnp.tanh(g_ffn[1]) * _L1_ffn_ref(_layernorm(x, axis=-1), L1_ffn_clip_x, L1_ffn_clip_down, L1_ffn_w_gate, L1_ffn_w_up, L1_ffn_w_down)
    x = x + jnp.tanh(g_xattn[2]) * _L2_xattn_ref(_layernorm(x, axis=-1), ctx_1024, ctx_1024, L2_xattn_W, L2_xattn_b, mask_BxS2_if0)
    x = x + jnp.tanh(g_ffn[2]) * _L2_ffn_ref(_layernorm(x, axis=-1), L2_ffn_w1, L2_ffn_b1, L2_ffn_w2, L2_ffn_b2)
    x = x + jnp.tanh(g_xattn[3]) * _L3_xattn_ref(_layernorm(x, axis=-1), ctx_1024, L3_xattn_Wq, L3_xattn_bq, L3_xattn_Wk, L3_xattn_bk, L3_xattn_Wv, L3_xattn_bv, L3_xattn_Wo, L3_xattn_bo)
    x = x + jnp.tanh(g_ffn[3]) * _L3_ffn_ref(_layernorm(x, axis=-1), L3_ffn_r1_w, L3_ffn_r1_b, L3_ffn_r2_w, L3_ffn_w_up, L3_ffn_w_down, L3_ffn_a_up, L3_ffn_a_down)
    return x

_drawn_inputs = setup_inputs


def setup_inputs(seed=0):
    import zlib

    import numpy as np

    out = dict(_drawn_inputs(seed))
    spreads = {'L0_ffn_be': (0.0, 0.1),
     'L0_ffn_ln_g': (1.0, 0.2),
     'L0_ffn_ln_b': (0.0, 0.1),
     'L1_xattn_ln_gamma': (1.0, 0.6),
     'L1_xattn_ln_beta': (0.0, 0.8),
     'L1_xattn_b_out': (0.0, 0.1),
     'L2_xattn_b': (0.0, 0.1),
     'L3_xattn_bq': (0.0, 0.724),
     'L3_xattn_bk': (0.0, 2.0),
     'L3_xattn_bv': (0.0, 0.279),
     'L3_xattn_bo': (0.0, 0.1),
     'L3_ffn_r1_b': (0.0, 0.8)}
    factors = {'g_ffn': 8.0,
     'L0_ffn_Wq': 8.0,
     'L0_ffn_Wk': 8.0,
     'L1_ffn_w_gate': 8.0,
     'L1_ffn_w_up': 8.0,
     'L1_ffn_w_down': 8.0,
     'L2_ffn_b1': 8.0,
     'L2_ffn_b2': 8.0,
     'L3_ffn_r1_w': 8.0,
     'L3_ffn_r2_w': 8.0,
     'L3_ffn_w_up': 8.0,
     'L3_ffn_w_down': 8.0,
     'L3_ffn_a_up': 38.884,
     'L3_ffn_a_down': 40.385}
    for name, (base, spread) in spreads.items():
        noise = np.random.default_rng([zlib.crc32(name.encode()), seed]).standard_normal(out[name].shape)
        drawn = base * np.exp(spread * noise) if base else spread * noise
        out[name] = jnp.asarray(drawn.astype(out[name].dtype))
    for name, factor in factors.items():
        out[name] = (out[name] * factor).astype(out[name].dtype)
    return out
```

```python
from contextlib import ExitStack

import numpy as np
import concourse.bass as bass
from concourse import mybir
from concourse.alu_op_type import AluOpType as ALU


F32 = mybir.dt.float32
BF16 = mybir.dt.bfloat16
U32 = mybir.dt.uint32
I32 = mybir.dt.int32
ACT = mybir.ActivationFunctionType
AX = mybir.AxisListType.X
RMAX = bass.bass_isa.ReduceOp.max
ds = bass.ds

P = 128
B, S, D = 8, 256, 128
NT = B * S // P
PARTS = 6
MASKED = -1.0e30
ROUND = 12582912.0
Q_SLOTS = ((0, 3), (3, 2), (5, 1))


class Heads:

    def __init__(self, dh, causal):
        self.dh, self.causal = dh, causal
        self.H = D // dh
        self.halves = self.H // 8
        self.units = 8
        self.per = self.H // self.units
        self.cols = P // self.per
        self.pad = PARTS * dh
        self.top = self.pad + 1
        self.end = self.pad + 3
        self.scale = float(dh) ** -0.5

    def order(self, s):
        H, last = self.H, self.halves - 1
        out = []
        a = s + 1 < B
        if s < 0:
            return ([("K0", 0), ("K0", 1), ("T", 0), ("T", 1)] + [("A", h) for h in range(H - 2)]
                    + [("K", 0), ("K", 1), ("A", H - 2), ("A", H - 1)])

        def batch(h):
            out.append(("B", h))
            if self.halves == 2 and h == 9:
                out.append(("O", 0))
            if self.halves == 2 and h == 11:
                out.append(("R", 0))
        if a:
            out.extend([("T", 0), ("T", 1)])
        out.extend([("B", 0), ("B", 1)])
        for h in range(H):
            if h == H - 2 and s + 2 < B:
                out.extend([("K", 0), ("K", 1)])
            if a:
                out.append(("A", h))
            if h == 1 and s > 0:
                out.append(("R", -1))
            if h + 2 < H:
                batch(h + 2)
            else:
                out.append(("V", h))
        out.append(("O", last))
        if not a:
            out.append(("R", last))
        return out


def flamingo(nc, T, out):
    with ExitStack() as ctx:
        def sb(name, shape, dt=F32, scope=ctx):
            return scope.enter_context(nc.sbuf_tensor(name, shape, dt))

        sems = {}

        def sem(name):
            if name not in sems:
                sems[name] = ctx.enter_context(nc.semaphore(name))
            return sems[name]

        bank = [ctx.enter_context(nc.psum_tensor(f"bank{i}", [P, 512], F32)) for i in range(8)]
        bank16 = [b[:, :].bitcast(BF16) for b in bank]

        ident = sb("ident", [P, P])
        identb = sb("identb", [P, P], BF16)
        cmaskf = sb("cmaskf", [P, 2, P])
        cmask = sb("cmask", [P, 2, P], BF16)
        bmean = sb("bmean", [P, P])
        ones = sb("ones", [P, P])
        gates = sb("gates", [P, 8])
        X = sb("X", [P, NT, D])
        Qf = sb("Qf", [P, NT, D])
        Kf = sb("Kf", [P, NT, D])
        V = sb("V", [P, NT * 16 * 32])
        OT = sb("OT", [P, 2, S])
        O = sb("O", [P, NT, D])
        Qst = sb("Qst", [P, 2, 2, 8, P], BF16)
        Kst = sb("Kst", [P, 2, 8, P], BF16)
        QT = sb("QT", [P, 8, S], BF16)
        KT = sb("KT", [P, 2, 8, S], BF16)
        QpT = sb("QpT", [P, 8, S], BF16)
        Pt = sb("Pt", [P, 4, 512])
        Mx = sb("Mx", [P, 2, 16])
        Rden = sb("Rden", [P, 2, 16])
        rest = sb("rest", [P, 2 * S])
        st1 = sb("st1", [P, 256])
        st2 = sb("st2", [P, 256])
        st3 = sb("st3", [P, 256])

        stage_done = sem("stage_done")
        dma_in = sem("dma_in")
        dma_out = sem("dma_out")
        full = {"A": sem("full_act"), "D": sem("full_dve")}
        evac = {"A": sem("evac_act"), "D": sem("evac_dve")}
        ln_ask, ln_answer = sem("ln_ask"), sem("ln_answer")
        dve_chain, act_chain, pool_chain = sem("dve_chain"), sem("act_chain"), sem("pool_chain")
        q_split, k_split = sem("q_split"), sem("k_split")
        tpA_full, tpA_free, tpK_free = sem("tpA_full"), sem("tpA_free"), sem("tpK_free")
        tpK_full = sem("tpK_full")
        tpQ_full, tpQ_free = sem("tpQ_full"), sem("tpQ_free")
        sm_full, max_done, max_in = sem("sm_full"), sem("max_done"), sem("max_in")
        st_full, exp_done, pv_done, norm_done = sem("st_full"), sem("exp_done"), sem("pv_done"), sem("norm_done")
        ot_free, rt_full = sem("ot_free"), sem("rt_full")
        mean_ask, mean_full = sem("mean_ask"), sem("mean_full")

        class Seat:
            def __init__(self, eng, chain=None):
                self.eng, self.chain = eng, chain
                self.links = 0
                self.barriers = 0
                self.uses = []
                self.emptied = {"A": 0, "D": 0}
                self.n = {}

            def count(self, name, k=1):
                self.n[name] = self.n.get(name, 0) + k
                return self.n[name]

            def link(self, ins):
                self.links += 1
                ins.then_inc(self.chain, 1)
                self.eng.wait_ge(self.chain, self.links)

            def barrier(self):
                self.barriers += 1
                self.eng.drain().then_inc(stage_done, 1)
                self.eng.wait_ge(stage_done, 5 * self.barriers)

            def settle(self):
                for who in "AD":
                    if self.emptied[who]:
                        self.eng.wait_ge(evac[who], self.emptied[who])

            def follow(self):
                for who in "AD":
                    past = [c for w, c in self.uses[:-3] if w == who]
                    if past:
                        self.eng.wait_ge(evac[who], past[-1])

            def next_bank(self, who):
                j = len(self.uses)
                self.emptied[who] += 1
                self.uses.append((who, self.emptied[who]))
                return j

            def fill(self, who):
                j = self.next_bank(who)
                if j >= 8:
                    w, c = self.uses[j - 8]
                    self.eng.wait_ge(evac[w], c)
                return j % 8

            def take(self, who, me):
                j = self.next_bank(who)
                if who != me:
                    return None
                self.eng.wait_ge(full[me], self.emptied[me])
                return j % 8

        def rstd_dve(v, var, n, eps, scale):
            d = v.eng
            v.link(d.tensor_scalar(var, var, scale, eps, ALU.mult, ALU.add))
            v.link(d.tensor_copy(st2[:, 0:n], var))
            d.drain().then_inc(ln_ask, 1)
            d.wait_ge(ln_answer, v.count("ln"))
            r, t = st3[:, 0:n], st2[:, 0:n]
            v.link(d.reciprocal(r, st2[:, 0:n]))
            v.link(d.tensor_tensor(t, r, r, ALU.mult))
            v.link(d.tensor_tensor(t, t, var, ALU.mult))
            v.link(d.tensor_scalar(t, t, -0.5, 1.5, ALU.mult, ALU.add))
            v.link(d.tensor_tensor(r, r, t, ALU.mult))

        def rstd_act(a, n):
            a.eng.wait_ge(ln_ask, a.count("ln"))
            a.eng.activation(st2[:, 0:n], st2[:, 0:n], ACT.Sqrt).then_inc(ln_answer, 1)

        def bc(ap, shape):
            return ap.to_broadcast(shape)

        def ln_dve(v, src, dst, tmp, eps):
            d = v.eng
            sh = [P, NT, D]
            m = st1[:, 0:NT]
            v.link(d.tensor_reduce(m, src, AX, ALU.add))
            v.link(d.tensor_scalar(m, m, -1.0 / D, None, ALU.mult))
            v.link(d.tensor_tensor(dst, src, bc(m.unsqueeze(2), sh), ALU.add))
            v.link(d.tensor_tensor(tmp, dst, dst, ALU.mult))
            v.link(d.tensor_reduce(m, tmp, AX, ALU.add))
            rstd_dve(v, m, NT, eps, 1.0 / D)
            v.link(d.tensor_tensor(dst, dst, bc(st3[:, 0:NT].unsqueeze(2), sh), ALU.mult))

        def stack(ap, L):
            return ap.rearrange("p t u (g c) -> p (t u g) c", g=L.per)

        def v_view(L):
            return V[:, 0:NT * L.H * 32].rearrange("p (t h e) -> p t h e", t=NT, e=32)

        def stack_fill(g, L, pad_bias=None):
            e = g.eng
            g.link(e.memset(Qst[:], 0.0))
            g.link(e.memset(Kst[:], 0.0))
            g.link(e.memset(V[:, 0:NT * L.H * 32], 0.0))
            g.link(e.memset(v_view(L)[:, :, :, L.dh:L.dh + 1], 1.0))
            for t in range(2):
                g.link(e.memset(stack(Qst[:, t], L)[:, :, L.pad:L.pad + 1], 1.0))
            g.link(e.memset(stack(Kst[:], L)[:, :, L.top:L.end], 1.0))

        def att_pool(g, L, base, pad=None, early=False):
            e = g.eng
            H2 = 2 * L.H
            r = rest[:, :].rearrange("p (x h d) -> p x h d", x=2, d=L.dh)
            assert H2 * L.dh == S

            for n in range(B):
                par = n % 2
                q = Qf[:, 2 * n:2 * n + 2, :].rearrange("p t (h d) -> p (t h) d", d=L.dh).unsqueeze(2)
                k = Kf[:, 2 * n:2 * n + 2, :].rearrange("p t (h d) -> p (t h) d", d=L.dh).unsqueeze(2)
                A = stack(Qst[:, par], L)[:, :, 0:L.pad].rearrange("p h (s d) -> p h s d", d=L.dh)
                C = stack(Kst[:], L)[:, :, 0:L.pad].rearrange("p h (s d) -> p h s d", d=L.dh)
                rq, rk = r[:, 0].unsqueeze(2), r[:, 1].unsqueeze(2)

                def wide(ap, times):
                    return bc(ap, [P, H2, times, L.dh])
                if n >= 1:
                    e.wait_ge(tpK_full, 2 * (base["N"] + n))
                e.tensor_copy(C[:, :, 5:6], k)
                g.link(e.tensor_copy(C[:, :, 0:4:3], wide(k, 2)))
                g.link(e.tensor_tensor(rk, k, C[:, :, 0:1], ALU.subtract))
                g.link(e.tensor_copy(C[:, :, 1:5:3], wide(rk, 2)))
                if pad is not None:
                    Kp = Kst[:].rearrange("p t u (g c) -> p t (u g) c", g=L.per)[:, :, :, L.pad:L.pad + 1]
                    g.link(e.tensor_copy(Kp, bc(pad[:, 2 * n:2 * n + 2].unsqueeze(2).unsqueeze(3),
                                                [P, 2, L.H, 1])))
                e.tensor_tensor(C[:, :, 2:3], rk, C[:, :, 1:2], ALU.subtract).then_inc(k_split, 1)
                if n == 0 and early:
                    g.barrier()
                if n >= 2:
                    e.wait_ge(tpQ_full, 2 * (base["N"] + n - 1))
                g.link(e.tensor_copy(A[:, :, 0:3], wide(q, 3)))
                g.link(e.tensor_tensor(rq, q, A[:, :, 0:1], ALU.subtract))
                g.link(e.tensor_copy(A[:, :, 3:5], wide(rq, 2)))
                e.tensor_tensor(A[:, :, 5:6], rq, A[:, :, 3:4], ALU.subtract).then_inc(q_split, 1)

        def att_steps(step):
            for s in range(-1, B):
                step(s, s % 2, s + 1 < B, s >= 0)

        def att_pe(p, L, base):
            pe = p.eng
            H, Nb, Hb, Ub = L.H, base["N"], base["H"], base["U"]
            Va = v_view(L)

            def rows(h, n):
                r0 = (h % L.per) * L.cols
                return slice(r0, r0 + n), h // L.per

            def transposes(src, b, done):
                for u in range(L.units):
                    last = pe.transpose(bank16[b][:, u * P:(u + 1) * P], src[:, u, :], identb[:, :])
                last.then_inc(done, 1)

            def scores_by_query(h, kt):
                rs, u = rows(h, L.pad + 1)
                o = bank[h % 2]
                for t in range(2):
                    w = P if (L.causal and t == 0) else S
                    last = pe.matmul(o[:, t * S:t * S + w], QT[rs, u, t * P:(t + 1) * P], kt[rs, u, 0:w],
                                     start=True, stop=not L.causal, skip_group_check=True)
                    if L.causal:
                        last = pe.matmul(o[:, t * S + w - P:t * S + w], identb[:, :], cmask[:, 0, :],
                                         start=False, stop=True, skip_group_check=True)
                last.then_inc(sm_full, 1)

            def scores_by_key(h, kt):
                rs, u = rows(h, L.end)
                o = bank[2 + h % 2]
                for t in range(2):
                    q0 = P if (L.causal and t == 1) else 0
                    last = pe.matmul(o[:, t * S:t * S + S - q0], kt[rs, u, t * P:(t + 1) * P],
                                     QpT[rs, u, q0:S], start=True, stop=not L.causal,
                                     skip_group_check=True)
                    if L.causal:
                        last = pe.matmul(o[:, t * S:t * S + P], identb[:, :], cmask[:, 1, :],
                                         start=False, stop=True, skip_group_check=True)
                last.then_inc(st_full, 1)

            def values(s, h):
                pe.wait_ge(exp_done, Hb + H * s + h + 1)
                u = Ub + L.halves * s + h // 8
                if h % 8 == 0 and u > 0:
                    pe.wait_ge(ot_free, u)
                r = slice(32 * (h % 4), 32 * (h % 4) + 32)
                c = S * (h % 8 // 4)
                for k in range(2):
                    q0 = P if (L.causal and k == 1) else 0
                    last = pe.matmul(bank[4][r, c + q0:c + S], Va[:, 2 * s + k, h, :],
                                     Pt[:, h % 4, k * S:k * S + S - q0], start=(k == 0), stop=(k == 1),
                                     skip_group_check=True)
                last.then_inc(pv_done, 1)

            def step(s, par, a, b):
                if b:
                    pe.wait_ge(max_in, 2 * (Nb + s + 1))
                    for t in range(2):
                        transposes(Qst[:, par, t], t, tpQ_full)
                    pe.wait_ge(tpQ_free, 2 * (Nb + s + 1))
                for kind, h in L.order(s):
                    if kind == "B":
                        if h >= 2:
                            pe.wait_ge(exp_done, Hb + H * s + h - 1)
                        scores_by_key(h, KT[:, par])
                        if h >= 2:
                            values(s, h - 2)
                    elif kind == "V":
                        values(s, h)
                    elif kind == "R":
                        u = Ub + L.halves * s + h
                        pe.wait_ge(ot_free, u + 1)
                        if u > 0:
                            pe.wait_ge(norm_done, 2 * u)
                        for t in range(2):
                            for k in range(2):
                                last = pe.transpose(bank[7][:, (2 * t + k) * P:(2 * t + k + 1) * P],
                                                    OT[:, k, t * P:(t + 1) * P], ident[:, :])
                        last.then_inc(rt_full, 1)
                    elif kind == "T":
                        if h == 0:
                            pe.wait_ge(q_split, Nb + s + 2)
                        pe.wait_ge(tpK_free, 2 * (Nb + s + 1) + h + 1)
                        transposes(Qst[:, 1 - par, h], 5 + h, tpA_full)
                    elif kind in ("K", "K0"):
                        n = Nb + s + (2 if kind == "K" else 1)
                        if h == 0:
                            pe.wait_ge(k_split, n + 1)
                        if n > 0:
                            pe.wait_ge(tpA_free, 2 * (n - 1) + h + 1)
                        transposes(Kst[:, h], 5 + h, tpK_full)
                    elif kind == "A":
                        if h == 0:
                            pe.wait_ge(tpA_free, 2 * (Nb + s + 2))
                            pe.wait_ge(tpK_free, 2 * (Nb + s + 2))
                        if h >= 2 or not isinstance(s, int) or s >= 0:
                            pe.wait_ge(max_done, Hb + H * (s + 1) + h - 1)
                        scores_by_query(h, KT[:, 1 - par])
            att_steps(step)

        def att_act(a, L, base):
            act = a.eng
            H, Nb, Hb, Ub = L.H, base["N"], base["H"], base["U"]

            def step(s, par, na, nb):
                for kind, h in L.order(s):
                    if kind == "O":
                        act.wait_ge(pv_done, Hb + H * s + 8 * (h + 1))
                        act.copy(OT[:].rearrange("p k q -> p (k q)"), bank[4][:, :]).then_inc(ot_free, 1)
                    elif kind == "B":
                        act.wait_ge(st_full, Hb + H * s + h + 1)
                        if h >= 4:
                            act.wait_ge(pv_done, Hb + H * s + h - 3)
                        w = 3 * P if L.causal else 2 * S
                        act.activation(Pt[:, h % 4, 0:w], bank[2 + h % 2][:, 0:w], ACT.Exp,
                                       scale=L.scale).then_inc(exp_done, 1)
                    elif kind == "T":
                        act.wait_ge(tpA_full, 2 * (Nb + s + 1) + h + 1)
                        act.copy(QT[:, :, h * P:(h + 1) * P],
                                 bank16[5 + h].rearrange("p (u q) -> p u q", u=8)).then_inc(tpA_free, 1)
            att_steps(step)

        def att_dve(v, L, base):
            d = v.eng
            H, Nb, Hb, Ub = L.H, base["N"], base["H"], base["U"]

            def keys_out(n, t):
                d.wait_ge(tpK_full, 2 * (Nb + n) + t + 1)
                d.tensor_copy(KT[:, n % 2, :, t * P:(t + 1) * P],
                              bank16[5 + t].rearrange("p (u q) -> p u q", u=8)).then_inc(tpK_free, 1)

            def step(s, par, na, nb):
                if nb:
                    for t in range(2):
                        d.wait_ge(tpQ_full, 2 * (Nb + s) + t + 1)
                        d.tensor_copy(QpT[:, :, t * P:(t + 1) * P],
                                      bank16[t].rearrange("p (u q) -> p u q", u=8)).then_inc(tpQ_free, 1)
                for kind, h in L.order(s):
                    n = s + 1
                    if kind == "K0":
                        keys_out(n, h)
                    if kind == "A":
                        d.wait_ge(sm_full, Hb + H * n + h + 1)
                        if L.causal:
                            d.tensor_reduce(Mx[:, 0, h:h + 1], bank[h % 2][:, 0:P], AX, ALU.max)
                            d.tensor_reduce(Mx[:, 1, h:h + 1], bank[h % 2][:, S:2 * S], AX,
                                            ALU.max).then_inc(max_done, 1)
                        else:
                            d.tensor_reduce(Mx[:, :, h], bank[h % 2][:, :].rearrange("p (t k) -> p t k", t=2),
                                            AX, ALU.max).then_inc(max_done, 1)
                    if kind == "A" and h == H - 1:
                        d.wait_ge(max_done, Hb + H * (n + 1))
                        St = Qst[:, 1 - par].rearrange("p t u (g c) -> p t (u g) c", g=L.per)
                        m = Mx[:, :, 0:H].unsqueeze(3)
                        d.tensor_scalar(St[:, :, :, L.top:L.top + 1], m, -1.0, None,
                                        ALU.mult).then_inc(max_in, 1)
                        d.wait_ge(max_in, 2 * (Nb + n) + 1)
                        d.scalar_tensor_tensor(out=St[:, :, :, L.top + 1:L.end], in0=m, scalar=-1.0,
                                               in1=St[:, :, :, L.top:L.top + 1], op0=ALU.mult,
                                               op1=ALU.subtract).then_inc(max_in, 1)
                        if s + 2 < B:
                            for t in range(2):
                                keys_out(s + 2, t)
                    if kind == "R":
                        u = Ub + L.halves * s + h
                        d.wait_ge(rt_full, u + 1)
                        o = bank[7][:, :].rearrange("p (t x e) -> p t x e", t=2, e=32)
                        R = Rden[:, :, 0:8].unsqueeze(3)
                        d.reciprocal(R, o[:, :, :, L.dh:L.dh + 1]).then_inc(norm_done, 1)
                        d.wait_ge(norm_done, 2 * u + 1)
                        n, half = s + h // L.halves, h % L.halves
                        y = O[:, 2 * n:2 * n + 2, 8 * L.dh * half:8 * L.dh * (half + 1)]
                        d.tensor_tensor(y.rearrange("p t (x d) -> p t x d", d=L.dh), o[:, :, :, 0:L.dh],
                                        bc(R, [P, 2, 8, L.dh]), ALU.mult).then_inc(norm_done, 1)
            att_steps(step)

        attentions = [Heads(8, True)] + [Heads(16, False)] * 6 + [Heads(8, True), Heads(8, False)]
        bases, nb_, hb_, ub_ = [], 0, 0, 0
        for L in attentions:
            bases.append({"N": nb_, "H": hb_, "U": ub_})
            nb_, hb_, ub_ = nb_ + B, hb_ + B * L.H, ub_ + B * L.halves

        x_rows = T["x"].rearrange("b (t p) c -> p (b t) c", p=P)
        N_IN = 6

        def setup_sp(s):
            e = s.eng
            e.dma_start(X[:], x_rows).then_inc(dma_in, 16)
            e.dma_start(ident[:], T["c_ident"]).then_inc(dma_in, 16)
            e.dma_start(cmaskf[:], T["c_mask"].rearrange("a p k -> p a k")).then_inc(dma_in, 16)
            e.dma_start(bmean[:], T["c_bmean"]).then_inc(dma_in, 16)
            e.dma_start(gates[:, 0:4], T["g_xattn"].rearrange("(a n) -> a n", a=1).to_broadcast([P, 4])).then_inc(dma_in, 16)
            e.dma_start(gates[:, 4:8], T["g_ffn"].rearrange("(a n) -> a n", a=1).to_broadcast([P, 4])).then_inc(dma_in, 16)
            s.count("in", N_IN)
            s.barrier()

        def setup_pool(g):
            loaded(g, N_IN)
            g.link(g.eng.memset(ones[:], 1.0))
            g.barrier()

        def setup_dve(v):
            v.eng.wait_ge(dma_in, 16 * v.count("in", N_IN))
            v.link(v.eng.tensor_copy(identb[:], ident[:]))
            v.link(v.eng.tensor_copy(cmask[:], cmaskf[:]))
            v.barrier()

        def setup_act(a):
            a.eng.wait_ge(dma_in, 16 * a.count("in", N_IN))
            a.eng.activation(gates[:], gates[:], ACT.Tanh)
            a.barrier()

        def loaded(seat, n):
            seat.eng.wait_ge(dma_in, 16 * seat.count("in", n))

        s0 = ExitStack()
        ctxS = sb("ctxS", [P, NT, D], scope=s0)
        tA = sb("tA", [P, NT, D], scope=s0)
        tB = sb("tB", [P, NT, D], scope=s0)
        tC = sb("tC", [P, NT, D], scope=s0)
        rope = sb("rope", [P, 2, 2, 4], scope=s0)
        s0.close()
        L0 = attentions[0]

        def rotate(seat, src, dst, tmp):
            e = seat.eng
            for j in range(2):
                def part(ap, o):
                    return ap.rearrange("p (b j) (h d z) -> p b j h d z", j=2, h=16, z=2)[:, :, j, :, :, o]
                sh = [P, B, 16, 4]
                xe, xo, ye, yo = part(src, 0), part(src, 1), part(dst, 0), part(dst, 1)
                c = bc(rope[:, 0, j, :].unsqueeze(1).unsqueeze(1), sh)
                s = bc(rope[:, 1, j, :].unsqueeze(1).unsqueeze(1), sh)
                t1 = tmp[:, 0:4, :].rearrange("p (a) (y h d) -> p (a y) h d", h=16, d=4)
                t2 = tmp[:, 4:8, :].rearrange("p (a) (y h d) -> p (a y) h d", h=16, d=4)
                e.tensor_tensor(t1, xe, c, ALU.mult)
                seat.link(e.tensor_tensor(t2, xo, s, ALU.mult))
                e.tensor_tensor(ye, t1, t2, ALU.subtract)
                seat.link(e.tensor_tensor(yo, xe, s, ALU.mult))
                seat.link(e.tensor_tensor(t1, xo, c, ALU.mult))
                seat.link(e.tensor_tensor(yo, yo, t1, ALU.add))

        def l0x_sp(s):
            e = s.eng
            e.dma_start(tA[:], T["x_heads"]).then_inc(dma_in, 16)
            e.dma_start(ctxS[:], T["ctx_heads"]).then_inc(dma_in, 16)
            e.dma_start(rope[:], T["c_rope"]).then_inc(dma_in, 16)
            s.count("in", 3)
            s.barrier()
            for b in range(B):
                e.wait_ge(norm_done, 2 * L0.halves * (b + 1))
                for j in range(2):
                    e.dma_start(T["s_heads"][b, :, j * P:(j + 1) * P, :].rearrange("h r d -> r h d"),
                                O[:, 2 * b + j, :].rearrange("p (h d) -> p h d", d=8)).then_inc(dma_out, 16)
            e.wait_ge(dma_out, 16 * s.count("out", 2 * B))
            e.dma_start(Qf[:], T["s_heads"].rearrange("b h s d -> (b h s d)").rearrange(
                "(t p c) -> p t c", p=P, c=D)).then_inc(dma_in, 16)
            s.count("in", 1)
            s.barrier()

        def l0x_pool(g):
            stack_fill(g, L0)
            loaded(g, 3)
            g.link(g.eng.tensor_copy(v_view(L0)[:, :, :, 0:8], ctxS[:].rearrange("p t (h d) -> p t h d", d=8)))
            rotate(g, ctxS[:], Kf[:], tB[:])
            g.barrier()
            att_pool(g, L0, bases[0])
            g.count("in", 1)
            g.barrier()

        def l0x_dve(v):
            d = v.eng
            loaded(v, 3)
            xs = tA[:].rearrange("p t (h d) -> p (t h) d", d=8)
            xc = tC[:].rearrange("p t (h d) -> p (t h) d", d=8)
            sq = O[:].rearrange("p t (h d) -> p (t h) d", d=8)
            sh = [P, 256, 8]
            d.tensor_reduce(st1[:], xs, AX, ALU.add).then_inc(mean_ask, 1)
            d.wait_ge(mean_full, 1)
            v.link(d.tensor_tensor(xc, xs, bc(bank[0][:, 0:256].unsqueeze(2), sh), ALU.subtract))
            v.link(d.tensor_tensor(sq, xc, xc, ALU.mult))
            d.tensor_reduce(st1[:], sq, AX, ALU.add).then_inc(mean_ask, 1)
            d.wait_ge(mean_full, 2)
            v.link(d.tensor_copy(st1[:], bank[1][:, 0:256]))
            rstd_dve(v, st1[:], 256, 1e-5, 1.0)
            v.link(d.tensor_tensor(xc, xc, bc(st3[:].unsqueeze(2), sh), ALU.mult))
            rotate(v, tC[:], Qf[:], tA[:])
            v.barrier()
            att_dve(v, L0, bases[0])
            loaded(v, 1)
            v.link(d.scalar_tensor_tensor(out=X[:], in0=Qf[:], scalar=gates[:, 0:1], in1=X[:],
                                          op0=ALU.mult, op1=ALU.add))
            v.barrier()

        def l0x_pe(p):
            p.count("in", 3)
            for k in range(2):
                p.eng.wait_ge(mean_ask, k + 1)
                p.eng.matmul(bank[k][:, 0:256], bmean[:], st1[:], start=True, stop=True).then_inc(mean_full, 1)
            p.barrier()
            att_pe(p, L0, bases[0])
            p.count("in", 1)
            p.barrier()

        def l0x_act(a):
            a.count("in", 4)
            rstd_act(a, 256)
            a.barrier()
            att_act(a, L0, bases[0])
            a.barrier()

        def transposes_pe(p, src, who="ADAD"):
            for c, w in enumerate(who):
                p.follow()
                b = p.fill(w)
                for k in range(4):
                    last = p.eng.transpose(bank[b][:, k * P:(k + 1) * P], src(4 * c + k), ident[:, :])
                last.then_inc(full[w], 1)

        def cols_pe(p, weight, srcT, who="ADAD"):
            for c, w in enumerate(who):
                p.follow()
                b = p.fill(w)
                p.eng.matmul(bank[b][0:weight.shape[1], :], weight, srcT[:, c * 512:(c + 1) * 512],
                             start=True, stop=True).then_inc(full[w], 1)

        def rows_pe(p, srcT, weight, who="ADAD"):
            for c, w in enumerate(who):
                p.follow()
                b = p.fill(w)
                for k in range(4):
                    t = 4 * c + k
                    last = p.eng.matmul(bank[b][:, k * P:(k + 1) * P], srcT[:, t * P:(t + 1) * P], weight,
                                        start=True, stop=True, skip_group_check=True)
                last.then_inc(full[w], 1)

        def empty(seat, me, put, who="ADAD"):
            for c, w in enumerate(who):
                b = seat.take(w, me)
                if b is not None:
                    put(c, bank[b][:, :]).then_inc(evac[me], 1)

        def put_plain(seat, me, dst):
            def put(c, b):
                o = dst[:, c * 512:(c + 1) * 512]
                return seat.eng.copy(o, b) if me == "A" else seat.eng.tensor_copy(o, b)
            return put

        def put_affine(seat, me, dst, scale, bias):
            def put(c, b):
                o = dst[:, c * 512:(c + 1) * 512]
                if me == "A":
                    return seat.eng.activation(o, b, ACT.Identity, scale=scale, bias=bias)
                return seat.eng.tensor_scalar(o, b, scale, bias, ALU.mult, ALU.add)
            return put

        def put_v(seat, me, L):
            def put(c, b):
                o = v_view(L)[:, 4 * c:4 * c + 4, :, 0:L.dh].rearrange("p t h d -> p (t h) d")
                i = b.rearrange("p (x d) -> p x d", d=L.dh)
                return seat.eng.copy(o, i) if me == "A" else seat.eng.tensor_copy(o, i)
            return put

        def flat(t):
            return t[:, :, :].rearrange("p t c -> p (t c)")

        s1 = ExitStack()
        nodes = sb("nodes", [P, 6, B * S], scope=s1)
        qcol = sb("qcol", [P, B * S], scope=s1)
        tcol = sb("tcol", [P, B * S], scope=s1)
        We = sb("We", [P, 20, D], scope=s1)
        Wn = sb("Wn", [P, 4, 6, D], scope=s1)
        beT = sb("beT", [P, 20], scope=s1)
        ew = sb("ew", [P, 18], scope=s1)
        ewbe = sb("ewbe", [P, 18], scope=s1)
        actw = sb("actw", [P, 6], scope=s1)
        lng = sb("lng", [P, 2, D], scope=s1)
        s1.close()

        NODES, edge = [], 0
        for c in range(6):
            nsrc = min(c + 1, 5)
            src = c - nsrc
            NODES.append(((edge + nsrc - 1, c), (edge, src + 1), (edge + nsrc // 2, src + nsrc // 2 + 1)))
            edge += nsrc

        def row_bc(name, n):
            return T[name].rearrange("(a n) -> a n", a=1).to_broadcast([P, n])

        qk_ready = sem("qk_ready")

        def l0f_sp(s):
            e = s.eng
            for dst, src in ((We[:], T["L0_ffn_We"].rearrange("e i o -> i e o")),
                             (Wn[:, 0], T["L0_ffn_Wq"].rearrange("e i o -> i e o")),
                             (Wn[:, 1], T["L0_ffn_Wk"].rearrange("e i o -> i e o")),
                             (Wn[:, 2], T["L0_ffn_Wv"].rearrange("e i o -> i e o")),
                             (Wn[:, 3], T["L0_ffn_Wo"].rearrange("e i o -> i e o")),
                             (beT[:], T["beT"]),
                             (ew[:], T["L0_ffn_ew"].rearrange("(a c) k -> a (c k)", a=1).to_broadcast([P, 18])),
                             (actw[:], row_bc("L0_ffn_act_w", 6)),
                             (lng[:, 0], row_bc("L0_ffn_ln_g", D)),
                             (lng[:, 1], row_bc("L0_ffn_ln_b", D))):
                e.dma_start(dst, src).then_inc(dma_in, 16)
            s.count("in", 10)
            s.barrier()
            for c in range(6):
                s.barrier()
                s.barrier()
            s.barrier()

        def l0f_pool(g):
            L = attentions[1]
            stack_fill(g, L)
            g.count("in", 10)
            g.barrier()
            for c in range(6):
                g.eng.wait_ge(qk_ready, 2 * (c + 1))
                att_pool(g, L, bases[1 + c], early=True)
                g.barrier()
            g.barrier()

        def l0f_pe(p):
            L = attentions[1]
            loaded(p, 10)
            p.barrier()
            transposes_pe(p, lambda t: Qf[:, t, :])
            for c in range(6):
                (eq, nq), (ek, nk), (ev, nv) = NODES[c]
                cols_pe(p, We[:, eq, :], nodes[:, nq])
                cols_pe(p, We[:, ek, :], nodes[:, nk])
                rows_pe(p, qcol, Wn[:, 0, c, :])
                rows_pe(p, tcol, Wn[:, 1, c, :])
                cols_pe(p, We[:, ev, :], nodes[:, nv])
                rows_pe(p, tcol, Wn[:, 2, c, :])
                p.settle()
                p.barrier()
                att_pe(p, L, bases[1 + c])
                p.barrier()
                transposes_pe(p, lambda t: O[:, t, :])
                cols_pe(p, Wn[:, 3, c, :], tcol, who="DDDD")
            transposes_pe(p, lambda t: nodes[:, 0, t * P:(t + 1) * P])
            p.barrier()

        def l0f_empty(seat, me, c, second):
            if not second:
                k = 3 * c
                empty(seat, me, put_affine(seat, me, qcol, ew[:, k:k + 1], ewbe[:, k:k + 1]))
                empty(seat, me, put_affine(seat, me, tcol, ew[:, k + 1:k + 2], ewbe[:, k + 1:k + 2]))
                empty(seat, me, put_plain(seat, me, flat(Qf)))
                empty(seat, me, put_plain(seat, me, flat(Kf)))
                seat.eng.drain().then_inc(qk_ready, 1)
                empty(seat, me, put_affine(seat, me, tcol, ew[:, k + 2:k + 3], ewbe[:, k + 2:k + 3]))
                empty(seat, me, put_v(seat, me, attentions[1]))
            else:
                empty(seat, me, put_plain(seat, me, tcol))

                def node(ci, b):
                    o = slice(ci * 512, (ci + 1) * 512)
                    return seat.eng.scalar_tensor_tensor(out=nodes[:, (c + 1) % 6, o], in0=b,
                                                         scalar=actw[:, c:c + 1], in1=qcol[:, o],
                                                         op0=ALU.mult, op1=ALU.add)
                empty(seat, me, node, who="DDDD")

        def l0f_act(a):
            rstd_act(a, NT)
            loaded(a, 10)
            a.barrier()
            empty(a, "A", put_plain(a, "A", nodes[:, 0]))
            for c in range(6):
                l0f_empty(a, "A", c, False)
                a.barrier()
                att_act(a, attentions[1], bases[1 + c])
                a.barrier()
                l0f_empty(a, "A", c, True)
            empty(a, "A", put_plain(a, "A", flat(Qf)))
            a.barrier()
            rstd_act(a, NT)

        def l0f_dve(v):
            d = v.eng
            ln_dve(v, X[:], Qf[:], O[:], 1e-5)
            loaded(v, 10)
            for c in range(6):
                for i, (e_, _) in enumerate(NODES[c]):
                    k = 3 * c + i
                    d.tensor_tensor(ewbe[:, k:k + 1], ew[:, k:k + 1], beT[:, e_:e_ + 1], ALU.mult)
            v.barrier()
            empty(v, "D", put_plain(v, "D", nodes[:, 0]))
            for c in range(6):
                l0f_empty(v, "D", c, False)
                v.barrier()
                att_dve(v, attentions[1], bases[1 + c])
                v.barrier()
                l0f_empty(v, "D", c, True)
            empty(v, "D", put_plain(v, "D", flat(Qf)))
            v.barrier()
            ln_dve(v, Qf[:], Qf[:], O[:], 1e-6)
            sh = [P, NT, D]
            v.link(d.tensor_tensor(Qf[:], Qf[:], bc(lng[:, 0].unsqueeze(1), sh), ALU.mult))
            v.link(d.tensor_tensor(Qf[:], Qf[:], bc(lng[:, 1].unsqueeze(1), sh), ALU.add))
            v.link(d.scalar_tensor_tensor(out=X[:], in0=Qf[:], scalar=gates[:, 4:5], in1=X[:],
                                          op0=ALU.mult, op1=ALU.add))

        def l0f_end(seat):
            seat.barrier()

        H1, DH1 = 16, 64
        s2 = ExitStack()
        xnT = sb("xnT", [P, B * S], scope=s2)
        w_q = sb("w_q", [P, H1 * DH1], scope=s2)
        w_kv = sb("w_kv", [P, 2 * H1 * DH1], scope=s2)
        w_out = sb("w_out", [P, 8, D], scope=s2)
        ctxb = sb("ctxb", [P, 2, S], scope=s2)
        qk = sb("qk", [P, 2, 8, 2 * S], scope=s2)
        qkb = sb("qkb", [P, 2, 2 * S], BF16, scope=s2)
        Vb = V[:, :].rearrange("p (a k h e) -> p a k h e", a=2, k=2, h=H1)
        AnT = sb("AnT", [P, 8, S], scope=s2)
        Esel = sb("Esel", [32, H1, P], BF16, scope=s2)
        NM = sb("NM", [P, 2, 2, H1], BF16, scope=s2)
        NMT = sb("NMT", [32, S], BF16, scope=s2)
        gb = sb("gb", [P, 2], scope=s2)
        brow = sb("brow", [P, D], scope=s2)
        g1 = sb("g1", [P, 1], scope=s2)
        s2.close()
        Hb1, Nb1 = hb_, nb_
        assert Nb1 == 9 * B

        prep_full, prep_act, prep_dve = sem("prep_full"), sem("prep_act"), sem("prep_dve")
        vch_full, vch_free, nm_full, nm_free = sem("vch_full"), sem("vch_free"), sem("nm_full"), sem("nm_free")
        eo_full, eo_free = sem("eo_full"), sem("eo_free")
        ctx_in = [sem("ctx_in_even"), sem("ctx_in_odd")]
        nmax_in, pair_done = sem("nmax_in"), sem("pair_done")
        l1_sm, l1_max, l1_st, l1_exp, l1_pv = sem("l1_sm"), sem("l1_max"), sem("l1_st"), sem("l1_exp"), sem("l1_pv")

        def order1(a, b):
            out = [("N", 0)] if b else []
            for j in range(8):
                if a:
                    out.append(("P", j))
                    if j % 2 == 0:
                        out.append(("V", j // 2))
                for i in range(2):
                    if b:
                        out.append(("B", 2 * j + i))
                    if a and j > 0:
                        out.append(("A", 2 * j - 2 + i))
            if b:
                out.append(("B", 16))
            if a:
                out += [("A", 14), ("A", 15), ("M", 0)]
            if b:
                out.append(("E", 0))
            return out

        def l1x_sp(s):
            e = s.eng
            for dst, src in ((w_q[:], T["L1_xattn_w_q"]), (w_kv[:], T["L1_xattn_w_kv"]),
                             (w_out[:], T["L1_xattn_w_out"].rearrange("(c p) o -> p c o", p=P)),
                             (gb[:, 0:1], T["L1_xattn_ln_gamma"].rearrange("(p a) -> p a", a=1)),
                             (gb[:, 1:2], T["L1_xattn_ln_beta"].rearrange("(p a) -> p a", a=1)),
                             (brow[:], row_bc("L1_xattn_b_out", D)),
                             (g1[:], row_bc("L1_xattn_gate", 1))):
                e.dma_start(dst, src).then_inc(dma_in, 16)
            s.count("in", 7)
            s.barrier()
            for b in range(B):
                if b >= 2:
                    e.wait_ge(prep_full, 8 * (b - 1))
                    e.wait_ge(vch_full, 4 * (b - 1))
                e.dma_start(ctxb[:, b % 2], T["ctxT"][:, b * S:(b + 1) * S]).then_inc(ctx_in[b % 2], 16)
            s.barrier()

        def l1x_pool(g):
            i32 = ident[0:32, 0:16].unsqueeze(2)
            j32 = ident[0:32, 16:32].unsqueeze(2)
            g.link(g.eng.tensor_tensor(Esel[:], bc(i32, [32, H1, P]), bc(j32, [32, H1, P]), ALU.add))
            g.link(g.eng.memset(V[:, :], 1.0))
            g.count("in", 7)
            g.barrier()
            g.barrier()

        def l1x_pe(p):
            pe = p.eng
            loaded(p, 7)
            p.barrier()
            transposes_pe(p, lambda t: Qf[:, t, :])
            p.settle()

            def values(s, par, h):
                j = h // 2
                pe.wait_ge(l1_exp, H1 * s + h + 1)
                if h % 2 == 0 and j >= 2:
                    pe.wait_ge(pair_done, 4 * (8 * s + j - 1))
                o = bank[4 if j % 2 == 0 else 7][:, S * (h % 2):S * (h % 2) + S]
                for k in range(2):
                    last = pe.matmul(o, Vb[:, par, k, h, :], Pt[:, h % 4, k * S:(k + 1) * S],
                                     start=(k == 0), stop=(k == 1), skip_group_check=True)
                last.then_inc(l1_pv, 1)

            def step(s, par, a, b):
                for kind, i in order1(a, b):
                    if kind == "N":
                        pe.wait_ge(nmax_in, 2 * (s + 1))
                        for t in range(2):
                            last = pe.transpose(bank16[6][0:32, t * P:(t + 1) * P],
                                                NM[:, t].rearrange("p a h -> p (a h)"), identb[:, :])
                        last.then_inc(nm_full, 1)
                    elif kind == "P":
                        if i == 0:
                            pe.wait_ge(ctx_in[1 - par], 8 * s + (16 if par == 0 else 24))
                            pe.wait_ge(eo_free, s + 1) if not isinstance(s, int) or s >= 0 else None
                        else:
                            pe.wait_ge(prep_act, 8 * (s + 1) + i)
                            pe.wait_ge(prep_dve, 8 * (s + 1) + i)
                        pe.matmul(bank[5][:, 0:S], w_q[:, i * P:(i + 1) * P], xnT[:, (s + 1) * S:(s + 2) * S],
                                  start=True, stop=True, skip_group_check=True)
                        pe.matmul(bank[5][:, S:2 * S], w_kv[:, i * P:(i + 1) * P], ctxb[:, 1 - par],
                                  start=True, stop=True, skip_group_check=True).then_inc(prep_full, 1)
                    elif kind == "V":
                        if i == 0 and b:
                            pe.wait_ge(nm_free, s + 1)
                        if i > 0:
                            pe.wait_ge(vch_free, 4 * (s + 1) + i)
                        t, c = i // 2, i % 2
                        pe.matmul(bank[6][:, :], ctxb[:, 1 - par, t * P:(t + 1) * P],
                                  w_kv[:, H1 * DH1 + c * 512:H1 * DH1 + (c + 1) * 512],
                                  start=True, stop=True).then_inc(vch_full, 1)
                    elif kind == "A":
                        if i % 2 == 0:
                            pe.wait_ge(prep_dve, 8 * (s + 1) + i // 2 + 1)
                        if i >= 2 or not isinstance(s, int) or s >= 0:
                            pe.wait_ge(l1_max, H1 * (s + 1) + i - 1)
                        r = slice(64 * (i % 2), 64 * (i % 2) + 64)
                        x = qkb[r, (i // 2) % 2]
                        for t in range(2):
                            last = pe.matmul(bank[i % 2][:, t * S:(t + 1) * S], x[:, t * P:(t + 1) * P],
                                             x[:, S:2 * S], start=True, stop=True, skip_group_check=True)
                        last.then_inc(l1_sm, 1)
                    elif kind == "B":
                        h = i
                        if h < H1:
                            if h == 0:
                                pe.wait_ge(nm_free, s + 1)
                            if h >= 2:
                                pe.wait_ge(l1_exp, H1 * s + h - 1)
                            r = slice(64 * (h % 2), 64 * (h % 2) + 64)
                            x = qk[r, par, h // 2]
                            for t in range(2):
                                o = bank[2 + h % 2][:, t * S:(t + 1) * S]
                                pe.matmul(o, x[:, S + t * P:S + (t + 1) * P], x[:, 0:S], start=True, stop=False,
                                          skip_group_check=True)
                                last = pe.matmul(o, Esel[:, h, :], NMT[:, :], start=False, stop=True,
                                                 skip_group_check=True)
                            last.then_inc(l1_st, 1)
                        if h >= 1:
                            values(s, par, h - 1)
                    elif kind == "E":
                        pe.wait_ge(pair_done, 32 * (s + 1))
                        if a:
                            pe.wait_ge(prep_act, 8 * (s + 2))
                        for t in range(2):
                            for c in range(8):
                                last = pe.matmul(bank[5][:, t * P:(t + 1) * P],
                                                 AnT[:, c, t * P:(t + 1) * P], w_out[:, c, :],
                                                 start=(c == 0), stop=(c == 7), skip_group_check=True)
                        last.then_inc(eo_full, 1)
            att_steps(step)
            p.barrier()

        def l1x_act(a):
            act = a.eng
            rstd_act(a, NT)
            rstd_act(a, NT)
            loaded(a, 7)
            a.link(act.activation(g1[:], g1[:], ACT.Tanh))
            a.barrier()
            empty(a, "A", put_affine(a, "A", xnT, gb[:, 0:1], gb[:, 1:2]))

            def step(s, par, na, nb):
                for kind, i in order1(na, nb):
                    if kind == "P":
                        act.wait_ge(prep_full, 8 * (s + 1) + i + 1)
                        act.copy(qk[:, 1 - par, i, :], bank[5][:, :]).then_inc(prep_act, 1)
                    elif kind == "V":
                        act.wait_ge(vch_full, 4 * (s + 1) + i + 1)
                        t, c = i // 2, i % 2
                        dst = Vb[:, 1 - par, t, 8 * c:8 * c + 8, :].rearrange("p h e -> p (h e)")
                        act.copy(dst.rearrange("p (q z d) -> p q z d", z=4, d=DH1)[:, :, 0:4:3, :],
                                 bank[6][:, :].rearrange("p (q z d) -> p q z d", z=2, d=DH1)).then_inc(vch_free, 1)
                    elif kind == "B" and i < H1:
                        act.wait_ge(l1_st, H1 * s + i + 1)
                        if i >= 4:
                            act.wait_ge(l1_pv, H1 * s + i - 3)
                        act.activation(Pt[:, i % 4, :], bank[2 + i % 2][:, :], ACT.Exp,
                                       scale=float(DH1) ** -0.5).then_inc(l1_exp, 1)
            att_steps(step)
            a.barrier()

        def l1x_dve(v):
            d = v.eng
            ln_dve(v, X[:], Qf[:], O[:], 1e-5)
            ln_dve(v, Qf[:], Qf[:], O[:], 1e-5)
            loaded(v, 7)
            v.barrier()
            empty(v, "D", put_affine(v, "D", xnT, gb[:, 0:1], gb[:, 1:2]))
            v.link(d.tensor_tensor(g1[:], g1[:], gates[:, 1:2], ALU.mult))
            v.link(d.tensor_scalar(brow[:], brow[:], g1[:, 0:1], None, ALU.mult))
            v.link(d.tensor_tensor(X[:], X[:], bc(brow[:].unsqueeze(1), [P, NT, D]), ALU.add))
            d.drain().then_inc(eo_free, 1)

            def norm(s, j):
                d.wait_ge(l1_pv, H1 * s + 2 * j + 2)
                o = bank[4 if j % 2 == 0 else 7]
                lo, hi = slice(0, 64), slice(64, P)
                n0 = 4 * (8 * s + j)
                if n0:
                    d.wait_ge(pair_done, n0)
                d.reciprocal(st1[lo, :], o[hi, 0:S]).then_inc(pair_done, 1)
                d.reciprocal(st1[hi, :], o[lo, S:2 * S]).then_inc(pair_done, 1)
                d.wait_ge(pair_done, n0 + 2)
                d.tensor_tensor(AnT[lo, j, :], o[lo, 0:S], st1[lo, :], ALU.mult).then_inc(pair_done, 1)
                d.tensor_tensor(AnT[hi, j, :], o[hi, S:2 * S], st1[hi, :], ALU.mult).then_inc(pair_done, 1)

            def step(s, par, na, nb):
                for kind, i in order1(na, nb):
                    if kind == "N":
                        d.wait_ge(nm_full, s + 1)
                        d.tensor_copy(NMT[:, :], bank16[6][0:32, 0:S]).then_inc(nm_free, 1)
                    elif kind == "P":
                        d.wait_ge(prep_act, 8 * (s + 1) + i + 1)
                        d.tensor_copy(qkb[:, i % 2, :], qk[:, 1 - par, i, :]).then_inc(prep_dve, 1)
                    elif kind == "A":
                        d.wait_ge(l1_sm, H1 * (s + 1) + i + 1)
                        d.tensor_reduce(Mx[:, :, i], bank[i % 2][:, :].rearrange("p (t k) -> p t k", t=2),
                                        AX, ALU.max).then_inc(l1_max, 1)
                    elif kind == "M":
                        d.wait_ge(l1_max, H1 * (s + 2))
                        d.tensor_scalar(NM[:, :, 0, :], Mx[:, :, 0:H1], -1.0, None, ALU.mult).then_inc(nmax_in, 1)
                        d.wait_ge(nmax_in, 2 * (s + 1) + 1)
                        d.scalar_tensor_tensor(out=NM[:, :, 1, :], in0=Mx[:, :, 0:H1], scalar=-1.0,
                                               in1=NM[:, :, 0, :], op0=ALU.mult,
                                               op1=ALU.subtract).then_inc(nmax_in, 1)
                    elif kind == "B" and i >= 2 and i % 2 == 0:
                        norm(s, i // 2 - 1)
                    elif kind == "E":
                        d.wait_ge(eo_full, s + 1)
                        d.scalar_tensor_tensor(out=X[:, 2 * s:2 * s + 2, :],
                                               in0=bank[5][:, 0:S].rearrange("p (t c) -> p t c", t=2),
                                               scalar=g1[:, 0:1], in1=X[:, 2 * s:2 * s + 2, :],
                                               op0=ALU.mult, op1=ALU.add).then_inc(eo_free, 1)
            att_steps(step)
            v.barrier()

        class Quant:
            def __init__(self, gated, fb, names, gate):
                self.gated, self.fb, self.names, self.gate = gated, fb, names, gate
                self.F = 4 * fb
                self.nw = 2 if gated else 1

        QUANTS = [Quant(True, 88, ("L1_ffn_w_gate", "L1_ffn_w_up", "L1_ffn_w_down"), 5),
                  Quant(False, P, ("L2_ffn_w1", None, "L2_ffn_w2"), 6)]
        assert QUANTS[0].F == 352 and QUANTS[1].F == 512

        s3 = ExitStack()
        xq = sb("xq", [P, NT, D], BF16, scope=s3)
        xqT = sb("xqT", [P, B * S], BF16, scope=s3)
        hT = sb("hT", [P, 4, B * S], scope=s3)
        hq = sb("hq", [P, 4, B * S], BF16, scope=s3)
        gact = sb("gact", [P, 2, 512], scope=s3)
        w1 = sb("w1", [P, 2, 4, D], scope=s3)
        w1q = sb("w1q", [P, 2, 4, D], BF16, scope=s3)
        w1T = sb("w1T", [P, 2, 4, P], BF16, scope=s3)
        w2 = sb("w2", [P, 512], scope=s3)
        w2q = sb("w2q", [P, 512], BF16, scope=s3)
        w2T = sb("w2T", [P, 4, P], BF16, scope=s3)
        sw1 = sb("sw1", [P, 2, 4], scope=s3)
        iw1 = sb("iw1", [P, 2, 4], scope=s3)
        sw2 = sb("sw2", [P, 2], scope=s3)
        b1c = sb("b1c", [P, 4], scope=s3)
        b2c = sb("b2c", [P, 1], scope=s3)
        sx = sb("sx", [P, 4], scope=s3)
        clip = sb("clip", [P, 2], scope=s3)
        most = sb("most", [P, 16], scope=s3)
        top1 = sb("top1", [P, 2], scope=s3)
        diag = sb("diag", [P, 2, P], scope=s3)
        orow = sb("orow", [P, 2, P], scope=s3)
        s3.close()
        all_ask, all_done = sem("all_ask"), sem("all_done")

        def ffn_sp(s, Q, lay):
            e = s.eng
            for dst, src in lay:
                e.dma_start(dst, src).then_inc(dma_in, 16)
            s.count("in", len(lay))
            for _ in range(4):
                s.barrier()

        def ffn_loads(Q):
            fb = Q.fb
            lay = [(w1[0:fb, i], T[Q.names[i]].rearrange("(k p) d -> p k d", p=fb)) for i in range(Q.nw)]
            lay.append((w2[:, 0:Q.F], T[Q.names[2]]))
            if Q.gated:
                lay += [(clip[:, 0:1], row_bc("L1_ffn_clip_x", 1)), (clip[:, 1:2], row_bc("L1_ffn_clip_down", 1))]
            else:
                lay += [(b1c[:], T["L2_b1"]), (b2c[:], T["L2_ffn_b2"].rearrange("(p a) -> p a", a=1))]
            return lay

        def ffn_pool(g, Q):
            g.count("in", len(ffn_loads(Q)))
            g.link(g.eng.memset(top1[:, 1:2], 0.0))
            g.barrier()
            for k in range(2):
                g.eng.wait_ge(all_ask, g.count("all"))
                g.eng.partition_all_reduce(top1[:, k:k + 1], top1[:, k:k + 1], P, bass.bass_isa.ReduceOp.max
                                           ).then_inc(all_done, 1)
                g.barrier()
            g.barrier()

        def round_clip(v, src, dst, tmp, lo, hi):
            d = v.eng
            v.link(d.tensor_scalar(tmp, src, ROUND, ROUND, ALU.add, ALU.subtract))
            v.link(d.tensor_scalar(dst, tmp, lo, hi, ALU.max, ALU.min))

        def act_scale(v, Q, k):
            d = v.eng
            m = top1[:, k:k + 1]
            if Q.gated:
                v.link(d.tensor_scalar(sx[:, 2 * k:2 * k + 1], m, clip[:, k:k + 1], 1.0 / 127.0, ALU.mult, ALU.mult))
            else:
                v.link(d.tensor_scalar(sx[:, 2 * k:2 * k + 1], m, 1e-8, 1.0 / 255.0, ALU.max, ALU.mult))
            v.link(d.reciprocal(sx[:, 2 * k + 1:2 * k + 2], sx[:, 2 * k:2 * k + 1]))

        def everywhere(v, k):
            v.eng.drain().then_inc(all_ask, 1)
            v.eng.wait_ge(all_done, v.count("all"))

        def ffn_dve(v, Q):
            d = v.eng
            fb, F, nw = Q.fb, Q.F, Q.nw
            lo, hi = (-128.0, 127.0) if Q.gated else (0.0, 255.0)
            top = {"apply_absolute_value": Q.gated}
            ln_dve(v, X[:], Qf[:], O[:], 1e-5)
            loaded(v, len(ffn_loads(Q)))
            v.barrier()
            v.link(d.tensor_reduce(top1[:, 0:1], flat(Qf), AX, ALU.max, **top))
            everywhere(v, 0)
            if Q.gated:
                v.link(d.tensor_scalar(clip[:], clip[:], 1.0, None, ALU.add))
                v.link(d.reciprocal(clip[:], clip[:]))
            act_scale(v, Q, 0)
            v.link(d.tensor_scalar(O[:], Qf[:], sx[:, 1:2], None, ALU.mult))
            round_clip(v, O[:], xq[:], O[:], lo, hi)
            W = w1[0:fb, 0:nw].rearrange("p a k d -> p (a k) d")
            Sw, Iw = (t[0:fb, 0:nw].rearrange("p a k -> p (a k)") for t in (sw1, iw1))
            v.link(d.tensor_reduce(Sw, W, AX, ALU.max, apply_absolute_value=True))
            v.link(d.tensor_scalar(Sw, Sw, 0.0 if Q.gated else 1e-8, 1.0 / 127.0, ALU.max, ALU.mult))
            v.link(d.reciprocal(Iw, Sw))
            v.link(d.tensor_tensor(W, W, bc(Iw.unsqueeze(2), [fb, 4 * nw, D]), ALU.mult))
            round_clip(v, W, w1q[0:fb, 0:nw].rearrange("p a k d -> p (a k) d"), W, -128.0, 127.0)
            v.link(d.tensor_reduce(sw2[:, 0:1], w2[:, 0:F], AX, ALU.max, apply_absolute_value=True))
            v.link(d.tensor_scalar(sw2[:, 0:1], sw2[:, 0:1], 0.0 if Q.gated else 1e-8, 1.0 / 127.0, ALU.max, ALU.mult))
            v.link(d.reciprocal(sw2[:, 1:2], sw2[:, 0:1]))
            v.link(d.tensor_scalar(w2[:, 0:F], w2[:, 0:F], sw2[:, 1:2], None, ALU.mult))
            round_clip(v, w2[:, 0:F], w2q[:, 0:F], w2[:, 0:F], -128.0, 127.0)
            v.link(d.tensor_scalar(Sw, Sw, sx[0:fb, 0:1], None, ALU.mult))
            if not Q.gated:
                v.link(d.reciprocal(iw1[:, 0], sw1[:, 0]))
                v.link(d.tensor_tensor(b1c[:], b1c[:], iw1[:, 0], ALU.mult))
                v.link(d.tensor_scalar(b1c[:], b1c[:], ROUND, ROUND, ALU.add, ALU.subtract))
                v.link(d.tensor_tensor(b1c[:], b1c[:], sw1[:, 0], ALU.mult))
            v.link(d.memset(most[:], 0.0))
            v.barrier()
            empty(v, "D", ffn_put_t(v, "D", Q), who=FFN_T)
            for c in range(4):
                for k in range(4):
                    i = 4 * c + k
                    o = hT[0:fb, k, c * 512:(c + 1) * 512]
                    v.take("A", "D")
                    if Q.gated:
                        b = v.take("D", "D")
                        d.wait_ge(evac["A"], v.emptied["A"])
                        d.scalar_tensor_tensor(out=o, in0=bank[b][0:fb, :], scalar=sw1[0:fb, 1, k:k + 1],
                                               in1=gact[0:fb, i % 2, :], op0=ALU.mult,
                                               op1=ALU.mult).then_inc(evac["D"], 1)
                        d.wait_ge(evac["D"], v.emptied["D"])
                    else:
                        d.wait_ge(evac["A"], v.emptied["A"])
                    last = d.tensor_reduce(most[0:fb, i:i + 1], o, AX, ALU.max, **top)
            v.link(last)
            v.link(d.tensor_reduce(top1[:, 1:2], most[:], AX, ALU.max))
            everywhere(v, 1)
            act_scale(v, Q, 1)
            g = gates[:, Q.gate:Q.gate + 1]
            v.link(d.tensor_scalar(sw2[:, 0:1], sw2[:, 0:1], sx[:, 2:3], None, ALU.mult))
            if not Q.gated:
                v.link(d.reciprocal(sw2[:, 1:2], sw2[:, 0:1]))
                v.link(d.tensor_tensor(b2c[:], b2c[:], sw2[:, 1:2], ALU.mult))
                v.link(d.tensor_scalar(b2c[:], b2c[:], ROUND, ROUND, ALU.add, ALU.subtract))
                v.link(d.tensor_tensor(b2c[:], b2c[:], sw2[:, 0:1], ALU.mult))
                v.link(d.tensor_scalar(diag[:, 1], ident[:], b2c[:, 0:1], g, ALU.mult, ALU.mult))
            v.link(d.tensor_scalar(diag[:, 0], ident[:], sw2[:, 0:1], g, ALU.mult, ALU.mult))
            for k in range(4):
                h = hT[0:fb, k]
                v.link(d.tensor_scalar(h, h, sx[0:fb, 3:4], None, ALU.mult))
                round_clip(v, h, hq[0:fb, k], h, lo, hi)
            v.barrier()

            def rows_of(c, b):
                return d.tensor_copy(orow[:].rearrange("p a c -> p (a c)"), b[:, 0:2 * P])
            empty(v, "D", rows_of, who="D")
            v.settle()
            if not Q.gated:
                v.link(d.tensor_tensor(X[:], X[:], bc(orow[:, 1].unsqueeze(1), [P, NT, D]), ALU.add))
            v.settle()

            def add_rows(c, b):
                t = O[:, 4 * c:4 * c + 4, :]
                v.link(d.tensor_tensor(t, b.rearrange("p (t c) -> p t c", c=D),
                                       bc(orow[:, 0].unsqueeze(1), [P, 4, D]), ALU.mult))
                return d.tensor_tensor(X[:, 4 * c:4 * c + 4, :], X[:, 4 * c:4 * c + 4, :], t, ALU.add)
            empty(v, "D", add_rows, who="DDDD")
            v.barrier()

        FFN_T = "ADAD"

        def ffn_put_t(seat, me, Q):
            fb = Q.fb
            cp = seat.eng.copy if me == "A" else seat.eng.tensor_copy

            def put(c, b):
                b = b.bitcast(BF16)
                if c < 2:
                    return cp(xqT[:, c * 1024:(c + 1) * 1024], b)
                if c == 2:
                    n = 4 * Q.nw * fb
                    return cp(w1T[:, 0:Q.nw, :, 0:fb].rearrange("p a k f -> p (a k) f"),
                              b[:, 0:n].rearrange("p (x f) -> p x f", f=fb))
                return cp(w2T[0:fb].rearrange("p k c -> p (k c)"), b[0:fb, 0:4 * P])
            return put

        def ffn_pe(p, Q):
            pe = p.eng
            fb, nw = Q.fb, Q.nw
            p.count("in", len(ffn_loads(Q)))
            p.barrier()
            p.barrier()
            p.settle()
            for c, w in enumerate(FFN_T):
                b = bank16[p.fill(w)]
                if c < 2:
                    for k in range(8):
                        last = pe.transpose(b[:, k * P:(k + 1) * P], xq[:, 8 * c + k, :], identb[:, :])
                elif c == 2:
                    for x in range(4 * nw):
                        last = pe.transpose(b[:, x * fb:(x + 1) * fb], w1q[0:fb, x // 4, x % 4, :],
                                            identb[0:fb, 0:fb])
                else:
                    for k in range(4):
                        last = pe.transpose(b[0:fb, k * P:(k + 1) * P], w2q[:, k * fb:(k + 1) * fb], identb[:, :])
                last.then_inc(full[w], 1)
            p.settle()
            for c in range(4):
                for k in range(4):
                    for i, w in enumerate("AD" if Q.gated else "A"):
                        b = bank[p.fill(w)]
                        pe.matmul(b[0:fb, :], w1T[:, i, k, 0:fb], xqT[:, c * 512:(c + 1) * 512],
                                  start=True, stop=True).then_inc(full[w], 1)
            p.barrier()
            p.settle()
            b = bank[p.fill("D")]
            for i in range(1 if Q.gated else 2):
                last = pe.matmul(b[:, i * P:(i + 1) * P], ones[:, :], diag[:, i], start=True, stop=True,
                                 skip_group_check=True)
            if Q.gated:
                last = pe.matmul(b[:, P:2 * P], ones[:, :], diag[:, 0], start=True, stop=True,
                                 skip_group_check=True)
            last.then_inc(full["D"], 1)
            for c in range(4):
                b = bank[p.fill("D")]
                for t in range(4):
                    for k in range(4):
                        last = pe.matmul(b[:, t * P:(t + 1) * P], hq[0:fb, k, (4 * c + t) * P:(4 * c + t + 1) * P],
                                         w2T[0:fb, k, :], start=(k == 0), stop=(k == 3), skip_group_check=True)
                last.then_inc(full["D"], 1)
            p.barrier()

        def ffn_act(a, Q):
            act = a.eng
            fb = Q.fb
            rstd_act(a, NT)
            loaded(a, len(ffn_loads(Q)))
            if Q.gated:
                a.link(act.activation(clip[:], clip[:], ACT.Exp, scale=-1.0))
            a.barrier()
            a.barrier()
            empty(a, "A", ffn_put_t(a, "A", Q), who=FFN_T)
            a.settle()
            for c in range(4):
                for k in range(4):
                    i = 4 * c + k
                    b = a.take("A", "A")
                    if Q.gated:
                        if i >= 2:
                            act.wait_ge(evac["D"], a.emptied["D"] - 1)
                        act.activation(gact[0:fb, i % 2, :], bank[b][0:fb, :], ACT.Silu,
                                       scale=sw1[0:fb, 0, k:k + 1]).then_inc(evac["A"], 1)
                        a.take("D", "A")
                    else:
                        act.activation(hT[:, k, c * 512:(c + 1) * 512], bank[b][:, :], ACT.Relu,
                                       scale=sw1[:, 0, k:k + 1], bias=b1c[:, k:k + 1]).then_inc(evac["A"], 1)
            a.barrier()
            for _ in range(5):
                a.take("D", "A")
            a.barrier()

        s4 = ExitStack()
        ocol = sb("ocol", [P, B * S], scope=s4)
        ctxT = sb("ctxT", [P, B * S], scope=s4)
        wx = sb("wx", [P, 4, D], scope=s4)
        bx = sb("bx", [P, 4, D], scope=s4)
        padi = sb("padi", [P, NT], I32, scope=s4)
        padf = sb("padf", [P, NT], scope=s4)
        s4.close()

        def x_loads(k):
            if k == 2:
                return [(Kf[:], T["ctx_1024"].rearrange("b (t p) c -> p (b t) c", p=P)),
                        (wx[:, 3], T["L2_WT"]), (bx[:, 3], row_bc("L2_xattn_b", D)), (padi[:], T["pad_cols"])]
            return ([(ctxT[:], T["ctxT"])] + [(wx[:, i], T[f"L3_W{n}T"]) for i, n in enumerate("qkvo")]
                    + [(bx[:, i], row_bc(f"L3_xattn_b{n}", D)) for i, n in enumerate("qkvo")])

        def x_sp(s, k):
            for dst, src in x_loads(k):
                s.eng.dma_start(dst, src).then_inc(dma_in, 16)
            s.count("in", len(x_loads(k)))
            for _ in range(3):
                s.barrier()

        def x_pool(g, k):
            L = attentions[5 + k]
            stack_fill(g, L)
            if k == 2:
                loaded(g, 4)
                g.link(g.eng.tensor_copy(v_view(L)[:, :, :, 0:L.dh], Kf[:].rearrange("p t (h d) -> p t h d", d=L.dh)))
                g.link(g.eng.tensor_scalar(padf[:], padi[:], 1.0, MASKED, ALU.is_equal, ALU.mult))
            else:
                g.eng.drain().then_inc(v_blank, 1)
                g.count("in", 9)
            g.barrier()
            att_pool(g, L, bases[5 + k], padf if k == 2 else None)
            g.barrier()
            g.barrier()

        def x_pe(p, k):
            loaded(p, len(x_loads(k)))
            if k == 3:
                p.eng.wait_ge(ln_ready, 1)
                transposes_pe(p, lambda t: Qf[:, t, :])
                rows_pe(p, ocol, wx[:, 0], who="DDDD")
                rows_pe(p, ctxT, wx[:, 1], who="DDDD")
                rows_pe(p, ctxT, wx[:, 2], who="DDDD")
            p.barrier()
            att_pe(p, attentions[5 + k], bases[5 + k])
            p.barrier()
            transposes_pe(p, lambda t: O[:, t, :])
            rows_pe(p, ocol, wx[:, 3], who="DDDD")
            p.barrier()

        def x_act(a, k):
            rstd_act(a, NT)
            a.count("in", len(x_loads(k)))
            if k == 3:
                empty(a, "A", put_plain(a, "A", ocol))
                for _ in range(3):
                    empty(a, "A", None, who="DDDD")
            a.barrier()
            att_act(a, attentions[5 + k], bases[5 + k])
            a.barrier()
            empty(a, "A", put_plain(a, "A", ocol))
            empty(a, "A", None, who="DDDD")
            a.barrier()

        ln_ready, v_blank = sem("ln_ready"), sem("v_blank")

        def x_dve(v, k):
            d = v.eng
            L = attentions[5 + k]
            ln_dve(v, X[:], Qf[:], O[:], 1e-5)
            loaded(v, len(x_loads(k)))
            if k == 3:
                d.drain().then_inc(ln_ready, 1)
                empty(v, "D", put_plain(v, "D", ocol))

                def biased(dst, i):
                    def put(c, b):
                        n = D // L.dh
                        if i == 2:
                            o = v_view(L)[:, 4 * c:4 * c + 4, :, 0:L.dh]
                            r = bx[:, i].rearrange("p (h d) -> p h d", d=L.dh).unsqueeze(1)
                            return d.tensor_tensor(o, b.rearrange("p (t h d) -> p t h d", t=4, d=L.dh),
                                                   bc(r, [P, 4, n, L.dh]), ALU.add)
                        return d.tensor_tensor(dst[:, 4 * c:4 * c + 4, :], b.rearrange("p (t c) -> p t c", t=4),
                                               bc(bx[:, i].unsqueeze(1), [P, 4, D]), ALU.add)
                    return put
                for i, dst in enumerate((Qf, Kf, V)):
                    if i == 2:
                        d.wait_ge(v_blank, 1)
                    empty(v, "D", biased(dst, i), who="DDDD")
            g = gates[:, k:k + 1]
            v.link(d.tensor_scalar(bx[:, 3], bx[:, 3], g, None, ALU.mult))
            v.link(d.tensor_tensor(X[:], X[:], bc(bx[:, 3].unsqueeze(1), [P, NT, D]), ALU.add))
            v.barrier()
            att_dve(v, L, bases[5 + k])
            v.barrier()
            empty(v, "D", put_plain(v, "D", ocol))

            def onto_x(c, b):
                x = X[:, 4 * c:4 * c + 4, :]
                return d.scalar_tensor_tensor(out=x, in0=b.rearrange("p (t c) -> p t c", t=4), scalar=g, in1=x,
                                              op0=ALU.mult, op1=ALU.add)
            empty(v, "D", onto_x, who="DDDD")
            v.barrier()

        E, G, CAP, HID = 32, 16, 80, 64
        assert CAP == int(1.25 * B * S / E)
        NTOK = B * S
        s5 = ExitStack()
        st = sb("st", [P, NT, 8], scope=s5)
        stT = sb("stT", [8, NTOK], scope=s5)
        xfT = sb("xfT", [P, NTOK], scope=s5)
        hr = sb("hr", [HID, NTOK], scope=s5)
        r1 = sb("r1", [P, HID], scope=s5)
        r1s = sb("r1s", [8, HID], scope=s5)
        r2 = sb("r2", [HID, E], scope=s5)
        iotaE = sb("iotaE", [P, E], scope=s5)
        iotaT = V[:, 0:NTOK]
        pr = sb("pr", [P, NT, E], scope=s5)
        hit = sb("hit", [P, 2, NT, E], scope=s5)
        t8 = sb("t8", [P, NT, 8], scope=s5)
        i8 = sb("i8", [P, NT, 8], U32, scope=s5)
        i2 = sb("i2", [P, 2, NT], scope=s5)
        col = sb("col", [P, 4, NT], scope=s5)
        XG = sb("XG", [P, NT, D + 1], scope=s5)
        sc = sb("sc", [E, 2, NTOK], scope=s5)
        vals = sb("vals", [E, 2, CAP], scope=s5)
        idx = sb("idx", [E, CAP], U32, scope=s5)
        slot = sb("slot", [CAP, 2, E], scope=s5)
        sloti = sb("sloti", [CAP, E], U32, scope=s5)
        xg = sb("xg", [CAP, 4, D + 1], scope=s5)
        xeT = sb("xeT", [P, 2, CAP], scope=s5)
        Wup = sb("Wup", [P, 2, 2, 512], scope=s5)
        Wdn = sb("Wdn", [P, 2, 2, 2, D], scope=s5)
        Aup = sb("Aup", [P, 2, 256], scope=s5)
        Adn = sb("Adn", [P, 2, D], scope=s5)
        sil = sb("sil", [P, 2, 3, CAP], scope=s5)
        he = sb("he", [P, 2, 3, CAP], scope=s5)
        wsl = sb("wsl", [CAP, 2], scope=s5)
        ye = sb("ye", [CAP, 2, D], scope=s5)
        yb = sb("yb", [CAP, 2, 3, D], BF16, scope=s5)
        sel = sb("sel", [CAP, 2, NTOK], BF16, scope=s5)
        s5.close()
        m_xt_full, m_xt_free = sem("m_xt_full"), sem("m_xt_free")
        m_up_full, m_sil, m_h = sem("m_up_full"), sem("m_sil"), sem("m_h")
        m_y_full, m_yb, m_sel, m_comb = sem("m_y_full"), sem("m_yb"), sem("m_sel"), sem("m_comb")
        m_w = [sem("m_w_even"), sem("m_w_odd")]
        m_g = [sem(f"m_gathered{i}") for i in range(4)]
        m_chain = sem("m_chain")
        xg_out = sem("xg_out")

        def moe_loads():
            return [(r1[:], T["L3_r1T"][0:D]), (r1s[0:6], T["L3_r1T"][D:D + 6]),
                    (r1s[6:7], T["L3_ffn_r1_b"].rearrange("(a n) -> a n", a=1)), (r2[:], T["L3_r2T"]),
                    (iotaE[:], T["c_iota"][:, 0:E].to_broadcast([P, E])),
                    (iotaT, T["c_iota"].to_broadcast([P, NTOK]))]

        def moe_sp(s):
            e = s.eng
            for dst, src in moe_loads():
                e.dma_start(dst, src).then_inc(dma_in, 16)
            s.count("in", 6)

            def load_group(g, par):
                for dst, src in ((Wup[:, par], T["L3_upT"][ds(g, 1)].rearrange("a p e j -> p (a e) j")),
                                 (Wdn[:, par].rearrange("p e k c -> p (e k) c"),
                                  T["L3_downT"][ds(g, 1)].rearrange("a p x c -> p (a x) c")),
                                 (Aup[:, par], T["L3_aupT"][ds(g, 1)].rearrange("a p j -> p (a j)")),
                                 (Adn[:, par], T["L3_adnT"][ds(g, 1)].rearrange("a p j -> p (a j)"))):
                    e.dma_start(dst, src).then_inc(m_w[par], 16)
            load_group(0, 0)
            load_group(1, 1)
            s.barrier()
            s.barrier()
            e.dma_start(T["s_rows"].rearrange("(t p) c -> p t c", p=P), XG[:]).then_inc(xg_out, 16)
            e.wait_ge(xg_out, 16)
            s.barrier()
            s.barrier()
            with e.Fori(0, (G - 2) // 2) as i:
                for par in range(2):
                    e.wait_ge(m_y_full, 2 * (2 * i + par + 1))
                    load_group(2 * i + par + 2, par)
            s.barrier()
            s.barrier()

        def moe_pool(g):
            e = g.eng
            g.count("in", 6)
            for _ in range(4):
                g.barrier()
            for k in range(E):
                if k >= 4:
                    e.wait_ge(m_yb, 4 * (k - 3))
                e.indirect_dma_start(out=xg[:, k % 4, :], out_offset=None, in_=T["s_rows"],
                                     in_offset=bass.IndirectOffsetOnAxis(ap=sloti[:, k:k + 1], axis=0)
                                     ).then_inc(m_g[k % 4], 16)
            g.barrier()
            g.barrier()

        def moe_pe(p):
            pe = p.eng
            loaded(p, 6)
            p.barrier()
            transposes_pe(p, lambda t: Qf[:, t, :])
            for c, w in enumerate("ADAD"):
                b = bank[p.fill(w)]
                for k in range(4):
                    last = pe.transpose(b[0:7, k * P:(k + 1) * P], st[:, 4 * c + k, 0:7], ident[:, :])
                last.then_inc(full[w], 1)
            p.settle()
            for c in range(4):
                b = bank[p.fill("A")]
                o = slice(c * 512, (c + 1) * 512)
                pe.matmul(b[0:HID, :], r1[:, :], xfT[:, o], start=True, stop=False)
                pe.matmul(b[0:HID, :], r1s[0:7, :], stT[0:7, o], start=False, stop=True).then_inc(full["A"], 1)
            p.settle()
            b = bank[p.fill("D")]
            for t in range(NT):
                last = pe.matmul(b[:, t * E:(t + 1) * E], hr[:, t * P:(t + 1) * P], r2[:, :], start=True,
                                 stop=True, skip_group_check=True)
            last.then_inc(full["D"], 1)
            p.barrier()
            for c, w in enumerate("ADAD"):
                b = bank[p.fill(w)]
                for k in range(4):
                    last = pe.transpose(b[0:E, k * P:(k + 1) * P], hit[:, 0, 4 * c + k, :], ident[:, :])
                last.then_inc(full[w], 1)
            p.barrier()
            b = bank[p.fill("D")]
            for k in range(2):
                last = pe.transpose(b[0:CAP, k * E:(k + 1) * E], vals[:, k, :], ident[0:E, 0:E])
            last.then_inc(full["D"], 1)
            p.settle()
            p.barrier()

            def turn(e, u):
                pe.wait_ge(m_g[u], 4 * (e - u) + 16)
                if not isinstance(e, int) or e >= 1:
                    pe.wait_ge(m_xt_free, e)
                pe.transpose(bank[4][:, 0:CAP], xg[:, u, 0:D], ident[0:CAP, 0:CAP]).then_inc(m_xt_full, 1)

            def up(e, u, par):
                q = u % 2
                if u % 2 == 0:
                    pe.wait_ge(m_w[par], 16 * (e - 2 * par) + 64)
                pe.wait_ge(m_xt_free, e + 1)
                o = bank[5 + q]
                for k in range(6):
                    w = (Wup[:, par, q, k * P:(k + 1) * P] if k < 2 else Aup[:, par, 0:P] if k == 2 else
                         Wup[:, par, q, (k - 1) * P:k * P] if k < 5 else Aup[:, par, P:2 * P])
                    last = pe.matmul(o[:, k * CAP:(k + 1) * CAP], w, xeT[:, q, :], start=True, stop=True,
                                     skip_group_check=True)
                last.then_inc(m_up_full, 1)

            def down(e, u, par):
                q = u % 2
                pe.wait_ge(m_h, 2 * e + 2)
                if not isinstance(e, int) or e >= 1:
                    pe.wait_ge(m_yb, 4 * e)
                for k in range(3):
                    w = Wdn[:, par, q, k] if k < 2 else Adn[:, par]
                    last = pe.matmul(bank[7][0:CAP, 0:D], he[:, q, k, :], w, start=(k == 0), stop=(k == 2))
                last.then_inc(m_y_full, 1)

            def combine(e, u, first=False, end=False):
                q = u % 2
                pe.wait_ge(m_yb, 4 * e + 4)
                pe.wait_ge(m_sel, e + 1)
                for c in range(4):
                    for k in range(3):
                        last = pe.matmul(bank[c][:, :], yb[:, q, k, :], sel[:, q, c * 512:(c + 1) * 512],
                                         start=(first and k == 0), stop=(end and k == 2), skip_group_check=True)
                last.then_inc(m_comb, 1)

            def step(e, u, par, first=False, left=4):
                down(e, u, par)
                if left > 1:
                    up(e + 1, (u + 1) % 4, ((u + 1) % 4) // 2)
                if left > 2:
                    turn(e + 2, (u + 2) % 4)
                combine(e, u, first, left == 1)
            turn(0, 0)
            up(0, 0, 0)
            turn(1, 1)
            for u in range(4):
                step(u, u, u // 2, first=(u == 0))
            with pe.Fori(1, E // 4 - 1) as i:
                for u in range(4):
                    step(4 * i + u, u, u // 2)
            for u in range(4):
                step(E - 4 + u, u, u // 2, left=4 - u)
            p.barrier()
            transposes_pe(p, lambda t: xfT[:, t * P:(t + 1) * P], who="DDDD")
            p.barrier()

        def moe_act(a):
            act = a.eng
            rstd_act(a, NT)
            act.wait_ge(ln_ask, a.count("ln"))
            act.activation(col[:, 0:2], col[:, 2:4], ACT.Sqrt).then_inc(ln_answer, 1)
            loaded(a, 6)
            a.barrier()
            empty(a, "A", put_plain(a, "A", xfT))
            for c, w in enumerate("ADAD"):
                b = a.take(w, "A")
                if b is not None:
                    act.copy(stT[0:7, c * 512:(c + 1) * 512], bank[b][0:7, :]).then_inc(evac["A"], 1)
            for c in range(4):
                b = a.take("A", "A")
                act.activation(hr[:, c * 512:(c + 1) * 512], bank[b][0:HID, :], ACT.Gelu).then_inc(evac["A"], 1)
            a.take("D", "A")
            act.wait_ge(ln_ask, a.count("ln"))
            act.activation(pr[:], pr[:], ACT.Exp).then_inc(ln_answer, 1)
            a.barrier()
            for c, w in enumerate("ADAD"):
                b = a.take(w, "A")
                if b is not None:
                    act.copy(sc[:, 0, c * 512:(c + 1) * 512], bank[b][0:E, :]).then_inc(evac["A"], 1)
            a.barrier()
            a.take("D", "A")
            a.barrier()

            def front(e, u):
                q = u % 2
                act.wait_ge(m_xt_full, e + 1)
                if not isinstance(e, int) or e >= 2:
                    act.wait_ge(m_up_full, e - 1)
                act.copy(xeT[:, q, :], bank[4][:, 0:CAP]).then_inc(m_xt_free, 1)
                act.wait_ge(m_up_full, e + 1)
                if not isinstance(e, int) or e >= 2:
                    act.wait_ge(m_h, 2 * e - 2)
                act.activation(sil[:, q], bank[5 + q][:, 0:3 * CAP].rearrange("p (k s) -> p k s", k=3),
                               ACT.Silu).then_inc(m_sil, 1)
            for u in range(4):
                front(u, u)
            with act.Fori(1, E // 4) as i:
                for u in range(4):
                    front(4 * i + u, u)
            a.barrier()
            empty(a, "A", None, who="DDDD")
            a.barrier()

        def moe_dve(v):
            d = v.eng
            ln_dve(v, X[:], Qf[:], O[:], 1e-5)
            sh = [P, NT, D]
            mean, dev = st[:, :, 0:1], col[:, 2, :]
            v.link(d.memset(st[:], 1.0))
            v.link(d.tensor_reduce(st[:, :, 0], Qf[:], AX, ALU.add))
            v.link(d.tensor_scalar(st[:, :, 0], st[:, :, 0], 1.0 / D, None, ALU.mult))
            v.link(d.tensor_tensor(O[:], Qf[:], bc(mean, sh), ALU.subtract))
            v.link(d.tensor_tensor(O[:], O[:], O[:], ALU.mult))
            v.link(d.tensor_reduce(col[:, 2], O[:], AX, ALU.add))
            v.link(d.tensor_scalar(col[:, 2], col[:, 2], 1.0 / (D - 1), None, ALU.mult))
            v.link(d.tensor_tensor(O[:], Qf[:], Qf[:], ALU.mult))
            v.link(d.tensor_reduce(col[:, 3], O[:], AX, ALU.add))
            d.drain().then_inc(ln_ask, 1)
            d.tensor_reduce(st[:, :, 2], Qf[:], AX, ALU.min)
            d.tensor_reduce(st[:, :, 3], Qf[:], AX, ALU.max)
            v.link(d.tensor_scalar(O[:], Qf[:], 1e-6, None, ALU.is_lt))
            v.link(d.scalar_tensor_tensor(out=O[:], in0=Qf[:], scalar=-1e-6, in1=O[:], op0=ALU.is_gt, op1=ALU.mult))
            v.link(d.tensor_reduce(st[:, :, 5], O[:], AX, ALU.add))
            v.link(d.tensor_scalar(st[:, :, 5], st[:, :, 5], 1.0 / D, None, ALU.mult))
            d.wait_ge(ln_answer, v.count("ln"))
            r = col[:, 0:2]
            s2_ = st2[:, 0:2 * NT].rearrange("p (a t) -> p a t", a=2)
            v.link(d.tensor_scalar(r, r, 1e-30, None, ALU.max))
            v.link(d.reciprocal(s2_, r))
            v.link(d.tensor_tensor(s2_, s2_, col[:, 2:4], ALU.mult))
            v.link(d.tensor_tensor(r, r, s2_, ALU.add))
            d.tensor_scalar(st[:, :, 1], col[:, 0], 0.5, None, ALU.mult)
            v.link(d.tensor_scalar(st[:, :, 4], col[:, 1], 0.5, None, ALU.mult))
            loaded(v, 6)
            v.barrier()
            empty(v, "D", put_plain(v, "D", xfT))
            for c, w in enumerate("ADAD"):
                b = v.take(w, "D")
                if b is not None:
                    d.tensor_copy(stT[0:7, c * 512:(c + 1) * 512], bank[b][0:7, :]).then_inc(evac["D"], 1)
            for c in range(4):
                v.take("A", "D")
            b = v.take("D", "D")
            lg = bank[b][:, :].rearrange("p (t e) -> p t e", e=E)
            she = [P, NT, E]
            m = col[:, 0]
            v.link(d.tensor_reduce(m, lg, AX, ALU.max))
            d.tensor_tensor(pr[:], lg, bc(m.unsqueeze(2), she), ALU.subtract).then_inc(evac["D"], 1)
            v.settle()
            d.drain().then_inc(ln_ask, 1)
            d.wait_ge(ln_answer, v.count("ln"))
            v.link(d.tensor_reduce(m, pr[:], AX, ALU.add))
            v.link(d.reciprocal(m, m))
            v.link(d.tensor_tensor(pr[:], pr[:], bc(m.unsqueeze(2), she), ALU.mult))
            for t in range(NT):
                last = d.max(t8[:, t, :], pr[:, t, :])
            v.link(last)
            for t in range(NT):
                last = d.max_index(i8[:, t, :], t8[:, t, :], pr[:, t, :])
            v.link(last)
            v.link(d.tensor_copy(i2[:], i8[:, :, 0:2].rearrange("p t a -> p a t")))
            for k in range(2):
                last = d.tensor_tensor(hit[:, k], bc(iotaE[:].unsqueeze(1), she),
                                       bc(i2[:, k].unsqueeze(2), she), ALU.is_equal)
            v.link(last)
            v.link(d.tensor_tensor(hit[:, 0], hit[:, 0], hit[:, 1], ALU.add))
            v.link(d.tensor_tensor(pr[:], pr[:], hit[:, 0], ALU.mult))
            v.link(d.scalar_tensor_tensor(out=hit[:, 0], in0=hit[:, 0], scalar=-1.0, in1=pr[:],
                                          op0=ALU.add, op1=ALU.add))
            v.link(d.tensor_tensor(m.unsqueeze(2), t8[:, :, 0:1], t8[:, :, 1:2], ALU.add))
            v.link(d.reciprocal(XG[:, :, D:D + 1], m.unsqueeze(2)))
            v.link(d.tensor_copy(XG[:, :, 0:D], Qf[:]))
            v.barrier()
            for c, w in enumerate("ADAD"):
                b = v.take(w, "D")
                if b is not None:
                    d.tensor_copy(sc[:, 0, c * 512:(c + 1) * 512], bank[b][0:E, :]).then_inc(evac["D"], 1)
            v.settle()
            for k in range(CAP // 8):
                o = slice(8 * k, 8 * k + 8)
                a_, b_ = sc[:, k % 2, :], sc[:, 1 - k % 2, :]
                v.link(d.max(vals[:, 0, o], a_))
                v.link(d.max_index(idx[:, o], vals[:, 0, o], a_))
                if k < CAP // 8 - 1:
                    v.link(d.match_replace(b_, vals[:, 0, o], a_, -3.0e38))
            v.link(d.tensor_scalar(vals[:, 0], vals[:, 0], 0.0, None, ALU.max))
            v.link(d.tensor_copy(vals[:, 1], idx[:]))
            v.barrier()
            b = v.take("D", "D")
            v.link(d.tensor_copy(slot[:], bank[b][0:CAP, 0:2 * E].rearrange("p (a e) -> p a e", a=2)))
            d.tensor_copy(sloti[:], slot[:, 1]).then_inc(evac["D"], 1)
            v.settle()
            v.barrier()

            def front(e, u):
                q = u % 2
                d.wait_ge(m_sil, e + 1)
                if not isinstance(e, int) or e >= 2:
                    d.wait_ge(m_y_full, e - 1)
                b = bank[5 + q][:, 3 * CAP:6 * CAP].rearrange("p (k s) -> p k s", k=3)
                d.tensor_tensor(he[:, q, 0:2], sil[:, q, 0:2], b[:, 0:2], ALU.mult).then_inc(m_h, 1)
                d.scalar_tensor_tensor(out=he[:, q, 2], in0=sil[:, q, 2], scalar=0.05, in1=b[:, 2],
                                       op0=ALU.mult, op1=ALU.mult).then_inc(m_h, 1)

            def choose(e, u):
                if not isinstance(e, int) or e >= 2:
                    d.wait_ge(m_comb, e - 1)
                d.tensor_scalar(sel[:, u % 2, :], iotaT[0:CAP, :], slot[:, 1, ds(e, 1)], None,
                                ALU.is_equal).then_inc(m_sel, 1)

            def back(e, u):
                q = u % 2
                d.wait_ge(m_g[u], 4 * (e - u) + 16)
                d.tensor_tensor(wsl[:, q:q + 1], xg[:, u, D:D + 1], slot[:, 0, ds(e, 1)], ALU.mult).then_inc(m_yb, 1)
                d.wait_ge(m_yb, 4 * e + 1)
                d.wait_ge(m_y_full, e + 1)
                if not isinstance(e, int) or e >= 2:
                    d.wait_ge(m_comb, e - 1)
                y = ye[:, q, :]
                z = ye[:, 1 - q, :]
                d.tensor_scalar(y, bank[7][0:CAP, 0:D], wsl[:, q:q + 1], None, ALU.mult).then_inc(m_chain, 1)
                d.wait_ge(m_chain, 2 * e + 1)
                d.tensor_copy(yb[:, q, 0], y).then_inc(m_yb, 1)
                d.wait_ge(m_yb, 4 * e + 2)
                d.tensor_tensor(z, y, yb[:, q, 0], ALU.subtract).then_inc(m_chain, 1)
                d.wait_ge(m_chain, 2 * e + 2)
                d.tensor_copy(yb[:, q, 1], z).then_inc(m_yb, 1)
                d.wait_ge(m_yb, 4 * e + 3)
                d.tensor_tensor(yb[:, q, 2], z, yb[:, q, 1], ALU.subtract).then_inc(m_yb, 1)

            def step(e, u, end=False):
                back(e, u)
                if not end:
                    front(e + 1, (u + 1) % 4)
                    choose(e + 1, (u + 1) % 4)
            front(0, 0)
            choose(0, 0)
            for u in range(4):
                step(u, u)
            with d.Fori(1, E // 4 - 1) as i:
                for u in range(4):
                    step(4 * i + u, u)
            for u in range(4):
                step(E - 4 + u, u, end=(u == 3))
            d.wait_ge(m_comb, E)
            for c in range(4):
                d.tensor_copy(xfT[:, c * 512:(c + 1) * 512], bank[c][:, :])
            v.barrier()
            g = gates[:, 7:8]

            def onto_x(c, b):
                x = X[:, 4 * c:4 * c + 4, :]
                return d.scalar_tensor_tensor(out=x, in0=b.rearrange("p (t c) -> p t c", t=4), scalar=g, in1=x,
                                              op0=ALU.mult, op1=ALU.add)
            empty(v, "D", onto_x, who="DDDD")
            v.barrier()

        def finish_sp(s):
            s.eng.dma_start(out.rearrange("b (t p) c -> p (b t) c", p=P), X[:]).then_inc(dma_out, 16)
            s.eng.wait_ge(dma_out, 16 * s.count("out", 1))

        block = ctx.enter_context(nc.Block())

        @block.sync
        def _(sp):
            s = Seat(sp)
            setup_sp(s)
            l0x_sp(s)
            l0f_sp(s)
            l0f_end(s)
            l1x_sp(s)
            ffn_sp(s, QUANTS[0], ffn_loads(QUANTS[0]))
            x_sp(s, 2)
            ffn_sp(s, QUANTS[1], ffn_loads(QUANTS[1]))
            x_sp(s, 3)
            moe_sp(s)
            finish_sp(s)

        @block.gpsimd
        def _(pool):
            g = Seat(pool, pool_chain)
            setup_pool(g)
            l0x_pool(g)
            l0f_pool(g)
            l0f_end(g)
            l1x_pool(g)
            ffn_pool(g, QUANTS[0])
            x_pool(g, 2)
            ffn_pool(g, QUANTS[1])
            x_pool(g, 3)
            moe_pool(g)

        @block.vector
        def _(dve):
            v = Seat(dve, dve_chain)
            setup_dve(v)
            l0x_dve(v)
            l0f_dve(v)
            l0f_end(v)
            l1x_dve(v)
            ffn_dve(v, QUANTS[0])
            x_dve(v, 2)
            ffn_dve(v, QUANTS[1])
            x_dve(v, 3)
            moe_dve(v)

        @block.tensor
        def _(pe):
            p = Seat(pe)
            loaded(p, N_IN)
            p.barrier()
            l0x_pe(p)
            l0f_pe(p)
            l0f_end(p)
            l1x_pe(p)
            ffn_pe(p, QUANTS[0])
            x_pe(p, 2)
            ffn_pe(p, QUANTS[1])
            x_pe(p, 3)
            moe_pe(p)

        @block.scalar
        def _(act):
            a = Seat(act, act_chain)
            setup_act(a)
            l0x_act(a)
            l0f_act(a)
            l0f_end(a)
            l1x_act(a)
            ffn_act(a, QUANTS[0])
            x_act(a, 2)
            ffn_act(a, QUANTS[1])
            x_act(a, 3)
            moe_act(a)


def constants():
    r = np.arange(P)
    above = r[:, None] < r[None, :]
    mask = np.stack([np.where(above, MASKED, 0.0), np.where(above.T, MASKED, 0.0)]).astype(np.float32)
    bmean = np.where(r[:, None] // 16 == r[None, :] // 16, 1.0 / D, 0.0).astype(np.float32)
    div = np.array([10000.0 ** (i / 8) for i in range(0, 8, 2)], np.float32)
    ang = (np.arange(S, dtype=np.float32)[:, None] / div).reshape(2, P, 4).transpose(1, 0, 2)
    rope = np.stack([np.cos(ang), np.sin(ang)], 1).astype(np.float32)
    return {"c_iota": np.arange(B * S, dtype=np.float32)[None, :], "c_ident": np.eye(P, dtype=np.float32), "c_mask": mask, "c_bmean": bmean, "c_rope": rope}


def kernel(**inputs):
    import numpy as _np
    import concourse.bacc as _bacc
    from concourse import mybir as _mybir
    from concourse.bass_utils import run_bass_kernel_spmd as _run

    nc = _bacc.Bacc("TRN2", target_bir_lowering=False, num_devices=1)
    laid = {k: _np.ascontiguousarray(v) for k, v in inputs.items()}

    def by_head(a):
        a = a.reshape(B, 16, 2, P, 8).transpose(3, 0, 2, 1, 4)
        return _np.ascontiguousarray(a).reshape(P, NT, D)

    laid["x_heads"] = by_head(laid["x"])
    laid["ctx_heads"] = by_head(laid["ctx_1024"])
    laid["ctxT"] = _np.ascontiguousarray(laid["ctx_1024"].reshape(-1, D).T)
    laid["beT"] = _np.ascontiguousarray(laid["L0_ffn_be"].T)
    laid["L2_b1"] = _np.ascontiguousarray(laid["L2_ffn_b1"].reshape(4, P).T)
    laid["L2_WT"] = _np.ascontiguousarray(laid["L2_xattn_W"].T)
    for n in "qkvo":
        laid[f"L3_W{n}T"] = _np.ascontiguousarray(laid[f"L3_xattn_W{n}"].T)
    laid["pad_cols"] = _np.ascontiguousarray(laid["mask_BxS2_if0"].reshape(NT, P).T)
    laid["L3_r1T"] = _np.ascontiguousarray(laid["L3_ffn_r1_w"].T)
    laid["L3_r2T"] = _np.ascontiguousarray(laid["L3_ffn_r2_w"].T)
    laid["L3_upT"] = _np.ascontiguousarray(laid["L3_ffn_w_up"].reshape(16, 2, 512, D).transpose(0, 3, 1, 2))
    laid["L3_downT"] = _np.ascontiguousarray(
        laid["L3_ffn_w_down"].reshape(16, 2, D, 2, P).transpose(0, 4, 1, 3, 2)).reshape(16, P, 4, D)
    laid["L3_aupT"] = _np.ascontiguousarray(laid["L3_ffn_a_up"].transpose(0, 2, 1))
    laid["L3_adnT"] = _np.ascontiguousarray(laid["L3_ffn_a_down"].transpose(0, 2, 1))
    laid.update(constants())
    arrays, T = {}, {}
    for name, a in laid.items():
        arrays[f"in_{name}"] = a
        T[name] = nc.dram_tensor(f"in_{name}", a.shape, _mybir.dt.from_np(a.dtype), kind="ExternalInput").ap()
    T["s_heads"] = nc.dram_tensor("s_heads", (B, 16, S, 8), F32, kind="Internal").ap()
    T["s_rows"] = nc.dram_tensor("s_rows", (B * S, D + 1), F32, kind="Internal").ap()
    out = nc.dram_tensor("x_out", (B, S, D), F32, kind="ExternalOutput").ap()
    flamingo(nc, T, out)
    r = _run(nc, [arrays], core_ids=[0])
    return r.results[0]["x_out"]
```
